# Optimizing a Trainium2 kernel written in Bass

```python
import numpy as np
import jax
import jax.numpy as jnp

def _softmax(x, axis=-1):
    return jax.nn.softmax(x, axis=axis)

def _gelu(x):
    return jax.nn.gelu(x, approximate=True)

def _silu(x):
    return jax.nn.silu(x)

def _sigmoid(x):
    return jax.nn.sigmoid(x)

def _layernorm(x, axis=-1, eps=1e-05):
    m = jnp.mean(x, axis=axis, keepdims=True)
    v = jnp.var(x, axis=axis, keepdims=True)
    return (x - m) / jnp.sqrt(v + eps)

def _scatter_add(tgt, idx, src, axis=0):
    return tgt.at[idx].add(src)

def _segment_sum(src, seg, n):
    return jax.ops.segment_sum(src, seg, n)
kernel_name = 'mk_seq_postln_d1_jaxref_r8_f12357'

def setup_inputs(seed: int=0):
    np.random.seed(seed)
    _w = jnp.asarray

    def _L0_attn_setup():
        import jax, jax.numpy as jnp
        import numpy as np
        D_MODEL = 256
        N_HEADS = 16
        HEAD_DIM = D_MODEL // N_HEADS
        B, T = (2, 256)
        key = jax.random.key(seed)
        ks = jax.random.split(key, 5)
        s = 0.02
        x = jax.random.normal(ks[0], (B, T, D_MODEL), dtype=jnp.float32)
        Wq = jax.random.normal(ks[1], (D_MODEL, D_MODEL), dtype=jnp.float32) * s
        Wk = jax.random.normal(ks[2], (D_MODEL, HEAD_DIM), dtype=jnp.float32) * s
        Wv = jax.random.normal(ks[3], (D_MODEL, HEAD_DIM), dtype=jnp.float32) * s
        Wo = jax.random.normal(ks[4], (D_MODEL, D_MODEL), dtype=jnp.float32) * s
        return {'x': x, 'Wq': Wq, 'Wk': Wk, 'Wv': Wv, 'Wo': Wo}
    _L0_attn_in = _L0_attn_setup()

    def _L0_ffn_setup():
        import jax, jax.numpy as jnp
        import numpy as np
        NUM_EXPERTS = 32
        TOP_K = 8
        SELECT_TOP_K = 4
        THRESHOLD = 0.5
        HIDDEN = 256
        D_FF = 96

        def _moe_forward(hidden_states, gate_weight, gate_up_proj, down_proj, similarity):
            B, S_len, H = hidden_states.shape
            E, K, Ssel = (NUM_EXPERTS, TOP_K, SELECT_TOP_K)
            x = hidden_states.reshape(-1, H)
            router_logits = x @ gate_weight.T
            router_probs = jax.nn.softmax(router_logits.astype(jnp.float32), axis=-1).astype(router_logits.dtype)
            router_top_value, router_indices = jax.lax.top_k(router_probs, K)
            routing_weights = router_top_value / jnp.clip(jnp.sum(router_top_value, axis=-1, keepdims=True), 1e-12, None)
            sim = similarity.astype(jnp.float32)
            sim = sim.at[jnp.arange(E), jnp.arange(E)].set(1.0)
            prim = router_indices[:, :Ssel]
            sec = router_indices[:, Ssel:]
            sim_cand = sim[sec[:, :, None], prim[:, None, :]]
            best_sim = jnp.max(sim_cand, axis=-1)
            best_i = jnp.argmax(sim_cand, axis=-1)
            prim_rep = jnp.broadcast_to(prim[:, None, :], sim_cand.shape)
            best_primary = jnp.take_along_axis(prim_rep, best_i[..., None], axis=-1)[..., 0]
            new_sec = jnp.where(best_sim < THRESHOLD, sec, best_primary) if THRESHOLD > 0.0 else best_primary
            rerouted_indices = jnp.concatenate([prim, new_sec], axis=1)
            combine = jnp.sum(jax.nn.one_hot(rerouted_indices, E, dtype=routing_weights.dtype) * routing_weights[..., None], axis=1)

            def expert_step(y, params):
                wgu, wd, cw = params
                gu = x @ wgu.T
                g, u = jnp.split(gu, 2, axis=-1)
                h = jax.nn.silu(g) * u
                y = y + h @ wd.T * cw[:, None]
                return (y, None)
            y0 = jnp.zeros_like(x)
            y, _ = jax.lax.scan(expert_step, y0, (gate_up_proj, down_proj, combine.T))
            return y.reshape(B, S_len, H)
        key = jax.random.key(seed)
        ks = jax.random.split(key, 5)
        hidden_states = jax.random.normal(ks[0], (4, 256, HIDDEN), dtype=jnp.float32)
        gate_weight = jax.random.normal(ks[1], (NUM_EXPERTS, HIDDEN), dtype=jnp.float32) * 0.02
        gate_up_proj = jax.random.normal(ks[2], (NUM_EXPERTS, 2 * D_FF, HIDDEN), dtype=jnp.float32) * 0.02
        down_proj = jax.random.normal(ks[3], (NUM_EXPERTS, HIDDEN, D_FF), dtype=jnp.float32) * 0.02
        similarity = jax.random.uniform(ks[4], (NUM_EXPERTS, NUM_EXPERTS), dtype=jnp.float32)
        return {'hidden_states': hidden_states, 'gate_weight': gate_weight, 'gate_up_proj': gate_up_proj, 'down_proj': down_proj, 'similarity': similarity}
    _L0_ffn_in = _L0_ffn_setup()
    _d = {'L0_attn_x': _L0_attn_in['x'], 'L0_attn_Wq': _L0_attn_in['Wq'], 'L0_attn_Wk': _L0_attn_in['Wk'], 'L0_attn_Wv': _L0_attn_in['Wv'], 'L0_attn_Wo': _L0_attn_in['Wo'], 'L0_ffn_gate_weight': _L0_ffn_in['gate_weight'], 'L0_ffn_gate_up_proj': _L0_ffn_in['gate_up_proj'], 'L0_ffn_down_proj': _L0_ffn_in['down_proj'], 'L0_ffn_similarity': _L0_ffn_in['similarity']}
    _x0 = _d['L0_attn_x']
    _d['L0_attn_x'] = jax.random.normal(jax.random.fold_in(jax.random.key(seed), 1), (4, 1024, 256), dtype=_x0.dtype)
    del _x0
    return _d

def reference(L0_attn_x, L0_attn_Wq, L0_attn_Wk, L0_attn_Wv, L0_attn_Wo, L0_ffn_gate_weight, L0_ffn_gate_up_proj, L0_ffn_down_proj, L0_ffn_similarity):

    def _L0_attn_ref(x, Wq, Wk, Wv, Wo):
        import jax, jax.numpy as jnp
        import numpy as np
        D_MODEL = 256
        N_HEADS = 16
        HEAD_DIM = D_MODEL // N_HEADS
        B, T = (2, 256)
        Bx, Tx, Dx = x.shape
        scale = HEAD_DIM ** (-0.5)
        q = (x @ Wq).reshape(Bx, Tx, N_HEADS, HEAD_DIM).transpose(0, 2, 1, 3)
        k = x @ Wk
        v = x @ Wv
        attn = jnp.einsum('bhqd,bkd->bhqk', q, k) * scale
        causal = jnp.triu(jnp.ones((Tx, Tx), dtype=bool), k=1)
        attn = jnp.where(causal[None, None], -jnp.inf, attn)
        weights = jax.nn.softmax(attn, axis=-1)
        weights = jnp.nan_to_num(weights)
        out = jnp.einsum('bhqk,bkd->bhqd', weights, v)
        out = out.transpose(0, 2, 1, 3).reshape(Bx, Tx, Dx)
        return out @ Wo

    def _L0_ffn_ref(hidden_states, gate_weight, gate_up_proj, down_proj, similarity):
        import jax, jax.numpy as jnp
        import numpy as np
        NUM_EXPERTS = 32
        TOP_K = 8
        SELECT_TOP_K = 4
        THRESHOLD = 0.5
        HIDDEN = 256
        D_FF = 96

        def _moe_forward(hidden_states, gate_weight, gate_up_proj, down_proj, similarity):
            B, S_len, H = hidden_states.shape
            E, K, Ssel = (NUM_EXPERTS, TOP_K, SELECT_TOP_K)
            x = hidden_states.reshape(-1, H)
            router_logits = x @ gate_weight.T
            router_probs = jax.nn.softmax(router_logits.astype(jnp.float32), axis=-1).astype(router_logits.dtype)
            router_top_value, router_indices = jax.lax.top_k(router_probs, K)
            routing_weights = router_top_value / jnp.clip(jnp.sum(router_top_value, axis=-1, keepdims=True), 1e-12, None)
            sim = similarity.astype(jnp.float32)
            sim = sim.at[jnp.arange(E), jnp.arange(E)].set(1.0)
            prim = router_indices[:, :Ssel]
            sec = router_indices[:, Ssel:]
            sim_cand = sim[sec[:, :, None], prim[:, None, :]]
            best_sim = jnp.max(sim_cand, axis=-1)
            best_i = jnp.argmax(sim_cand, axis=-1)
            prim_rep = jnp.broadcast_to(prim[:, None, :], sim_cand.shape)
            best_primary = jnp.take_along_axis(prim_rep, best_i[..., None], axis=-1)[..., 0]
            new_sec = jnp.where(best_sim < THRESHOLD, sec, best_primary) if THRESHOLD > 0.0 else best_primary
            rerouted_indices = jnp.concatenate([prim, new_sec], axis=1)
            combine = jnp.sum(jax.nn.one_hot(rerouted_indices, E, dtype=routing_weights.dtype) * routing_weights[..., None], axis=1)

            def expert_step(y, params):
                wgu, wd, cw = params
                gu = x @ wgu.T
                g, u = jnp.split(gu, 2, axis=-1)
                h = jax.nn.silu(g) * u
                y = y + h @ wd.T * cw[:, None]
                return (y, None)
            y0 = jnp.zeros_like(x)
            y, _ = jax.lax.scan(expert_step, y0, (gate_up_proj, down_proj, combine.T))
            return y.reshape(B, S_len, H)
        return _moe_forward(hidden_states, gate_weight, gate_up_proj, down_proj, similarity)
    x = L0_attn_x
    x = _layernorm(x + _L0_attn_ref(x, L0_attn_Wq, L0_attn_Wk, L0_attn_Wv, L0_attn_Wo), axis=-1)
    x = _layernorm(x + _L0_ffn_ref(x, L0_ffn_gate_weight, L0_ffn_gate_up_proj, L0_ffn_down_proj, L0_ffn_similarity), axis=-1)
    return x

_drawn_inputs = setup_inputs


def setup_inputs(seed=0):
    import zlib

    import numpy as np

    out = dict(_drawn_inputs(seed))
    spreads = {}
    factors = {'L0_attn_Wq': 8.0,
     'L0_attn_Wk': 8.0,
     'L0_attn_Wv': 6.094,
     'L0_attn_Wo': 6.234,
     'L0_ffn_gate_weight': 8.0,
     'L0_ffn_gate_up_proj': 8.0,
     'L0_ffn_down_proj': 8.0,
     'L0_ffn_similarity': 8.0}
    for name, (base, spread) in spreads.items():
        noise = np.random.default_rng([zlib.crc32(name.encode()), seed]).standard_normal(out[name].shape)
        drawn = base * np.exp(spread * noise) if base else spread * noise
        out[name] = jnp.asarray(drawn.astype(out[name].dtype))
    for name, factor in factors.items():
        out[name] = (out[name] * factor).astype(out[name].dtype)
    return out
```

```python
from contextlib import ExitStack

import concourse.bass as bass
from concourse import mybir

F32 = mybir.dt.float32
F32R = mybir.dt.float32r
BF16 = mybir.dt.bfloat16
U32 = mybir.dt.uint32
ALU = mybir.AluOpType
ACT = mybir.ActivationFunctionType
AX = mybir.AxisListType

P = 128
B, T, D = 4, 1024, 256
H, HD = 16, 16
KC = D // P
N = B * T
TILES = N // P
CH = 512
HALVES = T // CH
GH = 4
GPB = H // GH
GROUPS = B * GPB
KB = T // P
VW = 32
PARTS = 3
Q_PART = (0, 0, 0, 1, 1, 2)
K_PART = (0, 1, 2, 0, 1, 0)
SROWS = 16 * len(Q_PART)
MROWS = SROWS + PARTS
NEG = -1.0e30
SCALE = float(HD) ** -0.5

E, FF = 32, 96
TOPK, SEL = 8, 4
THRESH = 0.5
QE = 4
QUADS = E // QE
QF = QE * FF
QJ = QF // P
GUW = 2 * KC * QF
WQ = GUW + QJ * D
STAGE = WQ // 3
PIECES = QUADS * 3
EPS = 1e-5


def steps_of_group():
    return [(c, kb) for c in range(HALVES) for kb in range(KB // HALVES * (c + 1))]


def first_col(c, kb):
    return max(0, kb - c * (CH // P)) * P


def max_units():
    units = []
    for qt in range(KB):
        for k0 in range(0, (qt + 1) * P, CH):
            keys = min((qt + 1) * P - k0, CH)
            per = CH // keys
            for h0 in range(0, GH, per):
                units.append([(h, qt, k0, keys, (h - h0) * keys) for h in range(h0, min(h0 + per, GH))])
    return units


UNITS = max_units()
UNITS_A = [u for u in UNITS if u[0][1] < KB // 2]
UNITS_B = [u for u in UNITS if u[0][1] >= KB // 2]
A_LAG = 3
RING_A = len(UNITS_A) + A_LAG
RING = len(UNITS) + 2


def moe_block(
    nc, xT, x, Wq, Wk, Wv, Wo, gateT, guT, dT, sim, ident, iota, rankw, maskS, maskST, out,
):
    with ExitStack() as ctx:
        q_dram = nc.dram_tensor("q_parts", (PARTS, GROUPS, HD, HALVES, GH, CH), BF16, kind="Internal").ap()
        k_dram = nc.dram_tensor("k_parts", (PARTS, B, HD, T), BF16, kind="Internal").ap()
        v_dram = nc.dram_tensor("v_ones", (B, P, KB, VW), F32, kind="Internal").ap()
        o_dram = nc.dram_tensor("o_sums", (TILES, P, GPB, P), F32, kind="Internal").ap()
        project(nc, xT, Wq, Wk, Wv, q_dram, k_dram, v_dram)
        w_hi = ctx.enter_context(nc.sbuf_tensor("w_hi", [P, QUADS * WQ], F32R))
        w_lo = ctx.enter_context(nc.sbuf_tensor("w_lo", [P, QUADS * WQ], F32R))
        attend(nc, q_dram, k_dram, v_dram, o_dram, guT, dT, w_hi, w_lo, ident, maskS, maskST)
        experts(nc, o_dram, x, Wo, gateT, sim, ident, iota, rankw, w_hi, w_lo, out)


def project(nc, xT, Wq, Wk, Wv, q_dram, k_dram, v_dram):
    with ExitStack() as ctx:
        sb = lambda name, shape, dt: ctx.enter_context(nc.sbuf_tensor(name, shape, dt))
        ps = lambda name, shape: ctx.enter_context(nc.psum_tensor(name, shape, F32))
        sem = lambda name: ctx.enter_context(nc.semaphore(name))
        wq = sb("a_wq", [P, KC, D], F32)
        wk = sb("a_wk", [P, KC, HD], F32)
        wv = sb("a_wv", [P, KC, HD], F32)
        xt = [sb(f"a_xt{s}", [P, KC, CH], F32) for s in range(2)]
        parts = [sb(f"a_parts{s}", [P, 3, PARTS, CH], BF16) for s in range(2)]
        rest = [sb(f"a_rest{s}", [P, 3, CH], F32) for s in range(2)]
        vt = [sb(f"a_vt{s}", [P, CH // P, VW], F32) for s in range(2)]
        qk_ps = [[ps(f"a_ps{s}{j}", [P, CH]) for j in range(3)] for s in range(2)]
        v_ps = [ps(f"a_psv{s}", [P, CH]) for s in range(2)]
        w_loaded = sem("a_w_loaded")
        xt_loaded = [sem(f"a_xt_loaded{s}") for s in range(2)]
        mm_done = sem("a_mm_done")
        v_done = sem("a_v_done")
        p1_done = sem("a_p1_done")
        rest_done = sem("a_rest_done")
        p2_done = sem("a_p2_done")
        p3_done = sem("a_p3_done")
        vt_ready = sem("a_vt_ready")
        vt_set = sem("a_vt_set")
        stored = [sem(f"a_stored{s}") for s in range(2)]
        STORES = 16 * (4 * PARTS + PARTS + 1)
        rows = lambda j: P if j < 2 else HD

        with nc.Block() as block:

            @block.sync
            def _(sp):
                sp.dma_start(wq[:], Wq.rearrange("(c p) n -> p c n", p=P)).then_inc(w_loaded, 16)
                sp.dma_start(wk[:], Wk.rearrange("(c p) n -> p c n", p=P)).then_inc(w_loaded, 16)
                sp.dma_start(wv[:], Wv.rearrange("(c p) n -> p c n", p=P)).then_inc(w_loaded, 16)
                for s in range(2):
                    sp.dma_start(xt[s][:], xT[:, :, s * CH:(s + 1) * CH]).then_inc(xt_loaded[s], 16)

                def chunk(b, s, more):
                    n = b * 2 + s
                    if more:
                        sp.wait_ge(v_done, n + 1)
                        sp.dma_start(xt[s][:], xT[:, :, bass.ds(n * CH + 2 * CH, CH)]).then_inc(xt_loaded[s], 16)
                    sp.wait_ge(p2_done, n * 3 + 3)
                    sp.wait_ge(p3_done, n * 3 + 3)
                    for j in range(2):
                        for g in range(2):
                            for c in range(PARTS):
                                dst = q_dram[c, bass.ds(b * GPB + 2 * j + g, 1), :, s]
                                sp.dma_start(dst.rearrange("o d h t -> (o h) d t"),
                                             parts[s][64 * g:64 * g + 64, j, c, :]).then_inc(stored[s], 16)
                    for c in range(PARTS):
                        sp.dma_start(k_dram[c, bass.ds(b, 1), :, s * CH:(s + 1) * CH].rearrange("o d t -> (o d) t"),
                                     parts[s][0:HD, 2, c, :]).then_inc(stored[s], 16)
                    sp.wait_ge(vt_ready, n + 1)
                    tiles = CH // P
                    sp.dma_start(v_dram[bass.ds(b, 1), :, s * tiles:(s + 1) * tiles].rearrange("o p k w -> (o p) k w"),
                                 vt[s][:]).then_inc(stored[s], 16)

                with sp.Fori(0, B - 1) as b:
                    for s in range(2):
                        chunk(b, s, True)
                for s in range(2):
                    chunk(B - 1, s, False)
                for s in range(2):
                    sp.wait_ge(stored[s], B * STORES)

            @block.tensor
            def _(pe):
                pe.wait_ge(w_loaded, 48)

                def chunk(b, s, reused):
                    n = b * 2 + s
                    pe.wait_ge(xt_loaded[s], b * 16 + 16)
                    for j in range(3):
                        if reused:
                            pe.wait_ge(rest_done, n * 3 - 6 + j + 1)
                        w = wk if j == 2 else wq
                        c0 = 0 if j == 2 else j * P
                        for c in range(KC):
                            last = nc.tensor.matmul(qk_ps[s][j][0:rows(j), :], w[:, c, c0:c0 + rows(j)], xt[s][:, c, :],
                                                    start=(c == 0), stop=(c == KC - 1))
                        last.then_inc(mm_done, 1)
                    if reused:
                        pe.wait_ge(vt_ready, n - 1)
                    for k in range(CH // P):
                        for c in range(KC):
                            last = nc.tensor.matmul(v_ps[s][:, k * HD:(k + 1) * HD], xt[s][:, c, k * P:(k + 1) * P],
                                                    wv[:, c, :], start=(c == 0), stop=(c == KC - 1))
                    last.then_inc(v_done, 1)

                for s in range(2):
                    chunk(0, s, False)
                with pe.Fori(1, B) as b:
                    for s in range(2):
                        chunk(b, s, True)

            @block.scalar
            def _(act):
                def chunk(b, s, reused):
                    n = b * 2 + s
                    for j in range(3):
                        if reused and j == 0:
                            act.wait_ge(stored[s], b * STORES)
                        act.wait_ge(mm_done, n * 3 + j + 1)
                        nc.scalar.copy(parts[s][0:rows(j), j, 0, :], qk_ps[s][j][0:rows(j), :]).then_inc(p1_done, 1)
                    for j in range(3):
                        act.wait_ge(rest_done, n * 3 + j + 1)
                        nc.scalar.copy(parts[s][0:rows(j), j, 1, :], rest[s][0:rows(j), j, :]).then_inc(p2_done, 1)

                for s in range(2):
                    chunk(0, s, False)
                with act.Fori(1, B) as b:
                    for s in range(2):
                        chunk(b, s, True)

            @block.vector
            def _(dve):
                for s in range(2):
                    nc.vector.memset(vt[s][:, :, HD + 1:VW], 0.0)
                    nc.vector.memset(vt[s][:, :, HD:HD + 1], 1.0)

                def chunk(b, s, reused):
                    n = b * 2 + s
                    for j in range(3):
                        if reused:
                            dve.wait_ge(p3_done, n * 3 - 6 + j + 1)
                        dve.wait_ge(p1_done, n * 3 + j + 1)
                        nc.vector.tensor_tensor(rest[s][0:rows(j), j, :], qk_ps[s][j][0:rows(j), :],
                                                parts[s][0:rows(j), j, 0, :], ALU.subtract).then_inc(rest_done, 1)
                    if reused:
                        dve.wait_ge(stored[s], b * STORES)
                    dve.wait_ge(v_done, n + 1)
                    nc.vector.tensor_copy(vt[s][:, :, 0:HD], v_ps[s][:, 0:CH // P * HD].rearrange(
                        "p (k d) -> p k d", d=HD)).then_inc(vt_ready, 1)

                for s in range(2):
                    chunk(0, s, False)
                with dve.Fori(1, B) as b:
                    for s in range(2):
                        chunk(b, s, True)

            @block.gpsimd
            def _(pool):
                with pool.Fori(0, B) as b:
                    for s in range(2):
                        n = b * 2 + s
                        for j in range(3):
                            pool.wait_ge(p2_done, n * 3 + j + 1)
                            nc.gpsimd.tensor_tensor(parts[s][0:rows(j), j, 2, :], rest[s][0:rows(j), j, :],
                                                    parts[s][0:rows(j), j, 1, :], ALU.subtract).then_inc(p3_done, 1)


def attend(nc, q_dram, k_dram, v_dram, o_dram, guT, dT, w_hi, w_lo, ident_d, maskS_d, maskST_d):
    with ExitStack() as ctx:
        sb = lambda name, shape, dt: ctx.enter_context(nc.sbuf_tensor(name, shape, dt))
        ps = lambda name, shape: ctx.enter_context(nc.psum_tensor(name, shape, F32))
        sem = lambda name: ctx.enter_context(nc.semaphore(name))
        qs = [sb(f"b_qs{r}", [P, HALVES, GH, CH], BF16) for r in range(2)]
        ks = [sb(f"b_ks{r}", [P, T], BF16) for r in range(2)]
        vs = [sb(f"b_vs{r}", [P, KB, VW], F32) for r in range(2)]
        pr = [sb(f"b_pr{r}", [P, GH, CH], F32) for r in range(2)]
        osb = [sb(f"b_osb{c}", [P, CH], F32) for c in range(HALVES)]
        stage = [sb(f"b_stage{r}", [P, STAGE], F32) for r in range(2)]
        ident = sb("b_ident", [P, P], F32)
        masks = sb("b_masks", [P, 2, P], F32)
        identb = sb("b_identb", [P, P], BF16)
        maskS = sb("b_maskS", [P, P], BF16)
        maskST = sb("b_maskST", [P, P], BF16)
        mx = sb("b_mx", [P, 2, GH, GH], F32)
        mx2 = sb("b_mx2", [P, GH, GH], F32)
        mrow = sb("b_mrow", [16, 2, PARTS, P], BF16)
        mrest = sb("b_mrest", [16, 2, 2, P], F32)
        st_ps = [ps(f"b_st{r}", [P, 2, CH]) for r in range(2)]
        pv_ps = [ps(f"b_pv{c}", [P, CH]) for c in range(HALVES)]
        ring_ps = [ps(f"b_ring{r}", [P, CH]) for r in range(2)]

        consts = sem("b_consts")
        masks_ready = sem("b_masks_ready")
        q_loaded = [sem(f"b_q_loaded{r}") for r in range(2)]
        LOADS = 16 * (2 * len(Q_PART) + 1)
        st_ready = sem("b_st_ready")
        exp_done = sem("b_exp_done")
        pv_done = sem("b_pv_done")
        o_copied = sem("b_o_copied")
        o_stored = [sem(f"b_o_stored{c}") for c in range(HALVES)]
        ring_ready = sem("b_ring_ready")
        ring_free = sem("b_ring_free")
        mx_ready = sem("b_mx_ready")
        vec_chain = sem("b_vec_chain")
        mrow_ready = sem("b_mrow_ready")
        m_loaded = [sem(f"b_m_loaded{h}") for h in range(2)]
        staged = [sem(f"b_staged{r}") for r in range(2)]
        cut = sem("b_cut")
        STEPS = steps_of_group()
        NS = len(STEPS)
        share = lambda s: (s * (RING - 1) // (NS - 2)) if s <= NS - 2 else RING - 1

        def over_groups(eng, first, both, last):
            first(0, 0)
            with eng.Fori(0, GROUPS // 2 - 1) as i:
                both(i * 2 + 1, 1)
                both(i * 2 + 2, 0)
            last(GROUPS - 1, 1)

        with nc.Block() as block:

            @block.sync
            def _(sp):
                def load(G, r, reused):
                    if reused:
                        sp.wait_ge(pv_done, (G - 1) * NS)
                    for blk, c in enumerate(Q_PART):
                        sp.dma_start(qs[r][HD * blk:HD * blk + HD].rearrange("d c h t -> d (c h t)"),
                                     q_dram[c, bass.ds(G, 1)].rearrange("o d c h t -> (o d) (c h t)")).then_inc(q_loaded[r], 16)
                    for blk, c in enumerate(K_PART):
                        sp.dma_start(ks[r][HD * blk:HD * blk + HD, :],
                                     k_dram[c, bass.ds(G // GPB, 1)].rearrange("o d t -> (o d) t")).then_inc(q_loaded[r], 16)
                    sp.dma_start(vs[r][:], v_dram[bass.ds(G // GPB, 1)].rearrange("o p k w -> (o p) k w")).then_inc(q_loaded[r], 16)

                def m_rows(G, r, half):
                    sp.wait_ge(mrow_ready, G * 2 + half + 1)
                    for c in range(PARTS):
                        sp.dma_start(qs[r][SROWS + c:SROWS + c + 1, half], mrow[:, half, c, :]).then_inc(m_loaded[half], 16)

                def store(G, c):
                    sp.wait_ge(o_copied, G * HALVES + c + 1)
                    tiles = CH // P
                    dst = o_dram[bass.ds((G // GPB) * KB + c * tiles, tiles), :, bass.ds(G % GPB, 1)]
                    sp.dma_start(dst.rearrange("t r o x -> r (t o) x"),
                                 osb[c][:].rearrange("r (t x) -> r t x", x=P)).then_inc(o_stored[c], 16)

                sp.dma_start(ident[:], ident_d).then_inc(consts, 16)
                sp.dma_start(masks[:, 0], maskS_d).then_inc(consts, 16)
                sp.dma_start(masks[:, 1], maskST_d).then_inc(consts, 16)
                load(0, 0, False)
                load(1, 1, False)
                m_rows(0, 0, 0)

                m_rows(0, 0, 1)
                store(0, 0)
                m_rows(1, 1, 0)

                def group(G, r):
                    load(G + 1, 1 - r, True)
                    m_rows(G, r, 1)
                    store(G - 1, 1)
                    store(G, 0)
                    m_rows(G + 1, 1 - r, 0)

                with sp.Fori(0, GROUPS // 2 - 1) as i:
                    group(i * 2 + 1, 1)
                    group(i * 2 + 2, 0)
                m_rows(GROUPS - 1, 1, 1)
                store(GROUPS - 2, 1)
                store(GROUPS - 1, 0)
                store(GROUPS - 1, 1)
                for c in range(HALVES):
                    sp.wait_ge(o_stored[c], 16 * GROUPS)

            @block.tensor
            def _(pe):
                pe.wait_ge(masks_ready, 5)

                def ring_unit(G, r, u):
                    bank = ring_ps[u % 2]
                    if not (isinstance(G, int) and G * RING + u < 2):
                        pe.wait_ge(ring_free, G * RING + u - 1)
                    if u == RING_A or u == RING - 1:
                        half = 0 if u == RING_A else 1
                        if half:
                            pe.wait_ge(mx_ready, G + 1)
                        else:
                            pe.wait_ge(ring_free, G * RING + len(UNITS_A))
                        nc.tensor.transpose(bank[0:16, 0:P], mx[:, half].rearrange("p h q -> p (h q)"),
                                            ident[:]).then_inc(ring_ready, 1)
                        return
                    unit = UNITS[u if u < RING_A else u - 1]
                    for h, qt, k0, keys, col in unit:
                        c, q0 = divmod(qt * P, CH)
                        diag = k0 + keys == (qt + 1) * P
                        last = nc.tensor.matmul(bank[:, col:col + keys], qs[r][0:SROWS, c, h, q0:q0 + P],
                                                ks[r][0:SROWS, k0:k0 + keys], start=True, stop=not diag)
                        if diag:
                            last = nc.tensor.matmul(bank[:, col + keys - P:col + keys], identb[:], maskS[:],
                                                    start=False, stop=True)
                    last.then_inc(ring_ready, 1)

                def scores(G, r, s, hp):
                    c, kb = STEPS[s]
                    o = first_col(c, kb)
                    if not (isinstance(G, int) and G == 0 and s == 0):
                        pe.wait_ge(exp_done, G * 2 * NS + 2 * s + hp - 1)
                    if s == 0 and hp == 0:
                        pe.wait_ge(m_loaded[0], (G + 1) * 16 * PARTS)
                    if c == 1 and kb == 0 and hp == 0:
                        pe.wait_ge(m_loaded[1], (G + 1) * 16 * PARTS)
                    own = kb >= c * (CH // P)
                    for j in range(2):
                        h = 2 * hp + j
                        last = nc.tensor.matmul(st_ps[hp][:, j, o:CH], ks[r][0:MROWS, kb * P:(kb + 1) * P],
                                                qs[r][0:MROWS, c, h, o:CH], start=True, stop=not own)
                        if own:
                            last = nc.tensor.matmul(st_ps[hp][:, j, o:o + P], identb[:], maskST[:],
                                                    start=False, stop=True)
                    last.then_inc(st_ready, 1)

                def values(G, r, s):
                    c, kb = STEPS[s]
                    o = first_col(c, kb)
                    pe.wait_ge(exp_done, G * 2 * NS + 2 * s + 2)
                    if kb == 0 and not (isinstance(G, int) and G == 0):
                        pe.wait_ge(o_copied, G * HALVES + c - 1)
                    for h in range(GH):
                        last = nc.tensor.matmul(pv_ps[c][VW * h:VW * h + VW, o:CH], vs[r][:, kb, :],
                                                pr[s % 2][:, h, o:CH], start=(kb == 0),
                                                stop=(s == NS - 1 or STEPS[s + 1][0] != c))
                    last.then_inc(pv_done, 1)

                def group(G, r, more, fresh=False):
                    nxt = 1 - r
                    for s in range(NS):
                        scores(G, r, s, 0)
                        u0, u1 = (share(s - 2), share(s - 1)) if more and s >= 2 else (0, 0)
                        if s == 2 and more:
                            pe.wait_ge(q_loaded[nxt], loads_upto(G + 1))
                        mid = (u0 + u1) // 2
                        for u in range(u0, mid):
                            ring_unit(G + 1, nxt, u)
                        scores(G, r, s, 1)
                        for u in range(mid, u1):
                            ring_unit(G + 1, nxt, u)
                        if s == 1:
                            ring_unit(G, r, RING - 1)
                        if s >= 1:
                            values(G, r, s - 1)
                        elif not fresh:
                            values(G - 1, nxt, NS - 1)

                def loads_upto(G):
                    return (G // 2 + 1) * LOADS

                pe.wait_ge(q_loaded[0], LOADS)
                for u in range(RING - 1):
                    ring_unit(0, 0, u)
                over_groups(pe, lambda G, r: group(G, r, True, fresh=True), lambda G, r: group(G, r, True),
                            lambda G, r: group(G, r, False))
                values(GROUPS - 1, 1, NS - 1)

            @block.scalar
            def _(act):
                def group(G, r, fresh):
                    for s, (c, kb) in enumerate(STEPS):
                        o = first_col(c, kb)
                        for hp in range(2):
                            if hp == 0 and not (fresh and s < 2):
                                act.wait_ge(pv_done, G * NS + s - 1)
                            act.wait_ge(st_ready, G * 2 * NS + 2 * s + hp + 1)
                            nc.scalar.activation(pr[s % 2][:, 2 * hp:2 * hp + 2, o:CH], st_ps[hp][:, :, o:CH],
                                                 ACT.Exp, scale=SCALE).then_inc(exp_done, 1)
                        if s == KB // HALVES + 1:
                            copy_out(G, 0, fresh)
                        if s == 1 and not fresh:
                            copy_out(G - 1, 1, False)

                def copy_out(G, c, fresh):
                    if not fresh:
                        act.wait_ge(o_stored[c], G * 16)
                    act.wait_ge(pv_done, G * NS + (KB // HALVES if c == 0 else NS))
                    nc.scalar.copy(osb[c][:], pv_ps[c][:]).then_inc(o_copied, 1)

                over_groups(act, lambda G, r: group(G, r, True), lambda G, r: group(G, r, False),
                            lambda G, r: group(G, r, False))
                copy_out(GROUPS - 1, 1, False)

            @block.vector
            def _(dve):
                dve.wait_ge(consts, 48)
                nc.vector.tensor_copy(identb[:], ident[:]).then_inc(masks_ready, 1)
                nc.vector.tensor_copy(maskS[:], masks[:, 0]).then_inc(masks_ready, 1)
                nc.vector.tensor_copy(maskST[:], masks[:, 1]).then_inc(masks_ready, 1)
                for r in range(2):
                    nc.vector.memset(ks[r][SROWS:MROWS, :], 1.0).then_inc(masks_ready, 1)

                def ring_unit(G, u, chain):
                    bank = ring_ps[u % 2]
                    dve.wait_ge(ring_ready, G * RING + u + 1)
                    if u == RING_A or u == RING - 1:
                        half = 0 if u == RING_A else 1
                        if not (isinstance(G, int) and G == 0):
                            dve.wait_ge(m_loaded[half], G * 16 * PARTS)
                        neg, rest = mrow[:, half, 0, :], mrest[:, half, 0, :]
                        nc.vector.tensor_scalar(neg, bank[0:16, 0:P], -1.0, None, ALU.mult).then_inc(vec_chain, 1)
                        dve.wait_ge(vec_chain, chain + 1)
                        nc.vector.scalar_tensor_tensor(rest, bank[0:16, 0:P], -1.0, neg, ALU.mult,
                                                       ALU.subtract).then_inc(ring_free, 1)
                        dve.wait_ge(ring_free, G * RING + u + 1)
                        nc.vector.tensor_copy(mrow[:, half, 1, :], rest).then_inc(vec_chain, 1)
                        dve.wait_ge(vec_chain, chain + 2)
                        nc.vector.tensor_tensor(mrow[:, half, 2, :], rest, mrow[:, half, 1, :],
                                                ALU.subtract).then_inc(mrow_ready, 1)
                        return
                    unit = UNITS[u if u < RING_A else u - 1]
                    h0, qt, k0, keys, _ = unit[0]
                    n = len(unit)
                    half, q = divmod(qt, KB // 2)
                    dst = mx2[:, h0:h0 + n, q] if k0 else mx[:, half, h0:h0 + n, q]
                    nc.vector.tensor_reduce(dst, bank[:, 0:n * keys].rearrange("p (n k) -> p n k", k=keys),
                                            AX.X, ALU.max).then_inc(ring_free, 1)

                def next_group(G, chain):
                    for u in range(RING - 1):
                        ring_unit(G, u, chain)
                    dve.wait_ge(ring_free, G * RING + RING - 1)
                    nc.vector.tensor_tensor(mx[:, 1], mx[:, 1], mx2[:], ALU.max).then_inc(mx_ready, 1)

                next_group(0, 0)

                def group(G, more):
                    ring_unit(G, RING - 1, G * 4 + 2)
                    if more:
                        next_group(G + 1, G * 4 + 4)

                over_groups(dve, lambda G, r: group(G, True), lambda G, r: group(G, True),
                            lambda G, r: group(G, False))

            @block.gpsimd
            def _(pool):

                def fetch(j, r):
                    q, part = divmod(j, 3)
                    if part < 2:
                        src = guT[:, q, part * STAGE:(part + 1) * STAGE]
                    else:
                        src = dT[:, q, :]
                    pool.dma_start(stage[r][:], src).then_inc(staged[r], 16)

                fetch(0, 0)
                fetch(1, 1)
                for j in range(PIECES):
                    r = j % 2
                    at = slice(j * STAGE, (j + 1) * STAGE)
                    pool.wait_ge(staged[r], 16 * (j // 2 + 1))
                    nc.gpsimd.tensor_copy(w_hi[:, at], stage[r][:]).then_inc(cut, 1)
                    pool.wait_ge(cut, 2 * j + 1)
                    nc.gpsimd.tensor_tensor(w_lo[:, at], stage[r][:], w_hi[:, at].bitcast(F32),
                                            ALU.subtract).then_inc(cut, 1)
                    if j + 2 < PIECES:
                        pool.wait_ge(cut, 2 * j + 2)
                        fetch(j + 2, r)
                pool.wait_ge(cut, 2 * PIECES)


def experts(nc, o_dram, x_d, Wo, gateT, sim, ident_d, iota_d, rankw_d, w_hi, w_lo, out_d):
    with ExitStack() as ctx:
        sb = lambda name, shape, dt=F32: ctx.enter_context(nc.sbuf_tensor(name, shape, dt))
        ps = lambda name: ctx.enter_context(nc.psum_tensor(name, [P, CH], F32))
        sem = lambda name: ctx.enter_context(nc.semaphore(name))
        ident = sb("c_ident", [P, P])
        iota = sb("c_iota", [P, E])
        rankw = sb("c_rankw", [P, SEL])
        half_pow = sb("c_half_pow", [P, 1])
        ones = sb("c_ones", [P, P])
        wo_f = sb("c_wo_f", [P, KC, D])
        wo = [sb(f"c_wo{i}", [P, KC, D], F32R) for i in range(2)]
        gate_f = sb("c_gate_f", [P, KC, E])
        gate = [sb(f"c_gate{i}", [P, KC, E], F32R) for i in range(2)]
        simb = sb("c_simb", [P, P])
        ot = sb("c_ot", [P, GPB, P])
        xt = sb("c_xt", [P, D])
        pace = sb("c_pace", [P, 1])
        rsum = sb("c_rsum", [P, GPB, GH])
        attn = sb("c_attn", [P, D])
        aT = [sb(f"c_aT{i}", [P, KC, P], F32R) for i in range(2)]
        z = sb("c_z", [P, D])
        stats, mv, veps, rstd = sb("c_stats", [P, 6]), sb("c_mv", [P, 2]), sb("c_veps", [P, 1]), sb("c_rstd", [P, 1])
        x1n = sb("c_x1n", [P, D])
        xTn = [sb(f"c_xTn{i}", [P, KC, P], F32R) for i in range(2)]
        nmax, esum, re = sb("c_nmax", [P, 1]), sb("c_esum", [P, 1]), sb("c_re", [P, 1])
        ex, probs = sb("c_ex", [P, E]), sb("c_probs", [P, E])
        top, idx, idxf = sb("c_top", [P, TOPK]), sb("c_idx", [P, TOPK], U32), sb("c_idxf", [P, TOPK])
        wsum, wclip, winv, w8 = sb("c_wsum", [P, 1]), sb("c_wclip", [P, 1]), sb("c_winv", [P, 1]), sb("c_w8", [P, TOPK])
        oh = sb("c_oh", [P, TOPK, E])
        ohT = sb("c_ohT", [P, P])
        simrow = sb("c_simrow", [P, SEL, E])
        prod = sb("c_prod", [P, SEL, SEL, E])
        cand = sb("c_cand", [P, SEL, SEL])
        best, keep = sb("c_best", [P, SEL]), sb("c_keep", [P, SEL])
        eq, wt, wm, sel = sb("c_eq", [P, SEL, SEL]), sb("c_wt", [P, SEL, SEL]), sb("c_wm", [P, SEL]), sb("c_sel", [P, SEL, SEL])
        move, moved, added = sb("c_move", [P, SEL]), sb("c_moved", [P, SEL, SEL]), sb("c_added", [P, SEL])
        coef = sb("c_coef", [P, TOPK])
        prod2 = sb("c_prod2", [P, TOPK, E])
        x1 = sb("c_x1", [P, D])
        xT = [sb(f"c_xT{i}", [P, KC, P], F32R) for i in range(2)]
        cw = sb("c_cw", [P, E])
        th = [sb(f"c_th{r}", [P, QF]) for r in range(2)]
        hg = [sb(f"c_hg{r}", [P, QF]) for r in range(2)]
        hc = [sb(f"c_hc{r}", [P, QF]) for r in range(2)]
        hh = [sb(f"c_hh{r}", [P, QF]) for r in range(2)]
        hT = [[sb(f"c_hT{r}{i}", [P, QF], F32R) for i in range(2)] for r in range(2)]
        r2 = sb("c_r2", [P, D])
        stats2, mv2, veps2, rstd2 = sb("c_stats2", [P, 6]), sb("c_mv2", [P, 2]), sb("c_veps2", [P, 1]), sb("c_rstd2", [P, 1])
        ob = sb("c_ob", [P, D])
        g_ps = [ps(f"c_g{r}") for r in range(2)]
        u_ps = [ps(f"c_u{r}") for r in range(2)]
        hT_ps = [ps(f"c_hTp{r}") for r in range(2)]
        y_ps, m_ps = ps("c_y"), ps("c_m")

        consts = sem("c_consts")
        sim_zero = sem("c_sim_zero")
        set_up = sem("c_set_up")
        SETUP = 8
        CHAIN = 26
        g_done, u_done = sem("c_g_done"), sem("c_u_done")
        tanh_done = sem("c_tanh_done")
        a_done = sem("c_a_done")
        c_done = sem("c_c_done")
        h_done = sem("c_h_done")
        hT_done = sem("c_hT_done")
        hi_done, lo_done = sem("c_hi_done"), sem("c_lo_done")
        d_done = sem("c_d_done")
        ot_loaded, xt_loaded = sem("c_ot_loaded"), sem("c_xt_loaded")
        oT_done = sem("c_oT_done")
        attn_ready = sem("c_attn_ready")
        aT_done = sem("c_aT_done")
        aT_hi, aT_lo = sem("c_aT_hi"), sem("c_aT_lo")
        wo_done = sem("c_wo_done")
        z_done = sem("c_z_done")
        veps_ready, rstd_ready = sem("c_veps_ready"), sem("c_rstd_ready")
        x1n_ready = sem("c_x1n_ready")
        xT_done = sem("c_xT_done")
        xT_hi, xT_lo = sem("c_xT_hi"), sem("c_xT_lo")
        logits_done = sem("c_logits_done")
        nmax_ready, ex_done = sem("c_nmax_ready"), sem("c_ex_done")
        oh_ready = sem("c_oh_ready")
        ohT_done, ohT_ready = sem("c_ohT_done"), sem("c_ohT_ready")
        sim_done, simrow_ready = sem("c_sim_done"), sem("c_simrow_ready")
        prod_done = sem("c_prod_done")
        coef_ready = sem("c_coef_ready")
        prod2_done = sem("c_prod2_done")
        cw_ready = sem("c_cw_ready")
        rotated = sem("c_rotated")
        y_free = sem("c_y_free")
        veps2_ready, rstd2_ready = sem("c_veps2_ready"), sem("c_rstd2_ready")
        out_ready = sem("c_out_ready")
        out_stored = sem("c_out_stored")
        chain = sem("c_chain")

        def gu_cols(q, gu, c):
            at = q * WQ + (gu * KC + c) * QF
            return slice(at, at + QF)

        def d_cols(q, j):
            at = q * WQ + GUW + j * D
            return slice(at, at + D)

        with nc.Block() as block:

            @block.sync
            def _(sp):
                sp.wait_ge(sim_zero, 1)
                for s in range(SEL):
                    sp.dma_start(simb[E * s:E * s + E, E * s:E * s + E], sim).then_inc(consts, 16)
                for dst, src in ((ident, ident_d), (iota, iota_d), (rankw, rankw_d)):
                    sp.dma_start(dst[:], src).then_inc(consts, 16)
                sp.dma_start(wo_f[:], Wo.rearrange("(c p) n -> p c n", p=P)).then_inc(consts, 16)
                sp.dma_start(gate_f[:], gateT.rearrange("(c p) n -> p c n", p=P)).then_inc(consts, 16)

                def load_o(T):
                    sp.dma_start(ot[:], o_dram[bass.ds(T, 1)].rearrange("o p g x -> (o p) g x")).then_inc(ot_loaded, 16)

                def load_x(T):
                    sp.dma_start(xt[:], x_d[bass.ds(T * P, P), :]).then_inc(xt_loaded, 16)

                load_o(0)
                load_x(0)
                sp.wait_ge(oT_done, 1)
                load_o(1)
                sp.wait_ge(z_done, 1)
                load_x(1)
                with sp.Fori(0, TILES) as t:
                    nxt = (t + 2) % TILES
                    sp.wait_ge(oT_done, t + 2)
                    load_o(nxt)
                    sp.wait_ge(z_done, t + 2)
                    load_x(nxt)
                    sp.wait_ge(out_ready, t + 1)
                    sp.dma_start(out_d[bass.ds(t * P, P), :], ob[:]).then_inc(out_stored, 16)
                sp.wait_ge(ot_loaded, 16 * (TILES + 2))
                sp.wait_ge(xt_loaded, 16 * (TILES + 2))
                sp.wait_ge(out_stored, 16 * (TILES + 1))

            @block.tensor
            def _(pe):
                def passes(dst, lhs, rhs, chunks):
                    pairs = [(c, a, b) for c in chunks for a, b in ((0, 0), (0, 1), (1, 0))]
                    for i, (c, a, b) in enumerate(pairs):
                        last = nc.tensor.matmul(dst, lhs(a, c), rhs(b, c), start=(i == 0), stop=(i == len(pairs) - 1))
                    return last

                w = (w_hi, w_lo)

                def gate_up(n, q, T, first):
                    r = q % 2
                    if q == 0:
                        pe.wait_ge(rotated, T * 2 + 2)
                    if not first:
                        pe.wait_ge(h_done, n - 1)
                    passes(g_ps[r][:, 0:QF], lambda a, c: xT[a][:, c, :],
                           lambda b, c: w[b][:, gu_cols(q, 0, c)], range(KC)).then_inc(g_done, 1)
                    passes(u_ps[r][:, 0:QF], lambda a, c: xT[a][:, c, :],
                           lambda b, c: w[b][:, gu_cols(q, 1, c)], range(KC)).then_inc(u_done, 1)

                def turn(n, q):
                    r = q % 2
                    pe.wait_ge(h_done, n + 1)
                    for j in range(QJ):
                        last = nc.tensor.transpose(hT_ps[r][:, j * P:(j + 1) * P], hh[r][:, j * P:(j + 1) * P], ident[:])
                    last.then_inc(hT_done, 1)

                def down(n, q, t):
                    r = q % 2
                    pe.wait_ge(hi_done, n + 1)
                    pe.wait_ge(lo_done, n + 1)
                    if q == 0:
                        pe.wait_ge(y_free, t + 1)
                    for j in range(QJ):
                        for i, (a, b) in enumerate(((0, 0), (0, 1), (1, 0))):
                            last = nc.tensor.matmul(y_ps[:, 0:D], hT[r][a][:, j * P:(j + 1) * P], w[b][:, d_cols(q, j)],
                                                    start=(q == 0 and j == 0 and i == 0),
                                                    stop=(q == QUADS - 1 and j == QJ - 1 and i == 2))
                    last.then_inc(d_done, 1)

                def turn_outputs(T, first=False):
                    pe.wait_ge(ot_loaded, T * 16 + 16)
                    if not first:
                        pe.wait_ge(simrow_ready, T)
                    for g in range(GPB):
                        last = nc.tensor.transpose(m_ps[:, g * P:(g + 1) * P], ot[:, g, :], ident[:])
                    last.then_inc(oT_done, 1)

                def turn_attn(T):
                    pe.wait_ge(attn_ready, T + 1)
                    for c in range(KC):
                        last = nc.tensor.transpose(m_ps[:, c * P:(c + 1) * P], attn[:, c * P:(c + 1) * P], ident[:])
                    last.then_inc(aT_done, 1)

                def project_out(T):
                    pe.wait_ge(aT_lo, T + 1)
                    passes(m_ps[:, 0:D], lambda a, c: aT[a][:, c, :], lambda b, c: wo[b][:, c, :],
                           range(KC)).then_inc(wo_done, 1)

                def turn_x1(T):
                    pe.wait_ge(x1n_ready, T + 1)
                    for c in range(KC):
                        last = nc.tensor.transpose(m_ps[:, c * P:(c + 1) * P], x1n[:, c * P:(c + 1) * P], ident[:])
                    last.then_inc(xT_done, 1)

                def route(T):
                    pe.wait_ge(xT_lo, T + 1)
                    passes(m_ps[:, 0:E], lambda a, c: xTn[a][:, c, :], lambda b, c: gate[b][:, c, :],
                           range(KC)).then_inc(logits_done, 1)

                def turn_onehots(T):
                    pe.wait_ge(oh_ready, T + 1)
                    nc.tensor.transpose(m_ps[:, 0:P], oh[:, SEL:TOPK, :].rearrange("p k e -> p (k e)"),
                                        ident[:]).then_inc(ohT_done, 1)

                def similar(T):
                    pe.wait_ge(ohT_ready, T + 1)
                    nc.tensor.matmul(m_ps[:, 0:P], ohT[:], simb[:], start=True, stop=True).then_inc(sim_done, 1)

                pe.wait_ge(set_up, SETUP)
                turn_outputs(0, True)
                for piece in (turn_attn, project_out, turn_x1, route, turn_onehots, similar):
                    piece(0)
                gate_up(0, 0, 0, True)
                gate_up(1, 1, 0, True)
                turn(0, 0)
                with pe.Fori(0, TILES) as t:
                    for s in range(QUADS):
                        n = t * QUADS + s + 2
                        gate_up(n, (s + 2) % QUADS, t + (s + 2) // QUADS, False)
                        if s == 1:
                            turn_attn(t + 1)
                        if s == 3:
                            route(t + 1)
                        if s == 5:
                            similar(t + 1)
                        turn(n - 1, (s + 1) % QUADS)
                        down(n - 2, s, t)
                        if s == 0:
                            turn_outputs(t + 1)
                        if s == 1:
                            project_out(t + 1)
                        if s == 2:
                            turn_x1(t + 1)
                        if s == 4:
                            turn_onehots(t + 1)

            @block.scalar
            def _(act):
                def tanh(n, r, first):
                    act.wait_ge(g_done, n + 1)
                    if not first:
                        act.wait_ge(a_done, n - 1)
                    nc.scalar.activation(th[r][:], g_ps[r][:, 0:QF], ACT.Tanh, scale=0.5).then_inc(tanh_done, 1)

                def high(n, r):
                    act.wait_ge(hT_done, n + 1)
                    nc.scalar.copy(hT[r][0][:], hT_ps[r][:, 0:QF]).then_inc(hi_done, 1)

                def attn_high(T):
                    act.wait_ge(aT_done, T + 1)
                    nc.scalar.copy(aT[0][:].rearrange("p c n -> p (c n)"), m_ps[:, 0:D]).then_inc(aT_hi, 1)

                def x1_high(T):
                    act.wait_ge(xT_done, T + 1)
                    nc.scalar.copy(xTn[0][:].rearrange("p c n -> p (c n)"), m_ps[:, 0:D]).then_inc(xT_hi, 1)

                def exps(T):
                    act.wait_ge(nmax_ready, T + 1)
                    nc.scalar.activation(ex[:], m_ps[:, 0:E], ACT.Exp, bias=nmax[:], accum_out=esum[:]).then_inc(ex_done, 1)

                def onehots_out(T):
                    act.wait_ge(ohT_done, T + 1)
                    nc.scalar.copy(ohT[:], m_ps[:, 0:P]).then_inc(ohT_ready, 1)

                def similar_out(T):
                    act.wait_ge(sim_done, T + 1)
                    nc.scalar.copy(simrow[:].rearrange("p s e -> p (s e)"), m_ps[:, 0:P]).then_inc(simrow_ready, 1)

                def rotate(T):
                    act.wait_ge(xT_lo, T + 1)
                    for i in range(2):
                        nc.scalar.copy(xT[i][:], xTn[i][:].bitcast(F32)).then_inc(rotated, 1)

                for piece in (attn_high, x1_high, exps, onehots_out, similar_out, rotate):
                    piece(0)
                tanh(0, 0, True)
                tanh(1, 1, True)
                high(0, 0)
                with act.Fori(0, TILES) as t:
                    for s in range(QUADS):
                        n = t * QUADS + s + 2
                        tanh(n, s % 2, False)
                        if s == 1:
                            attn_high(t + 1)
                        if s == 5:
                            act.wait_ge(u_done, n + 1)
                            rotate(t + 1)
                            similar_out(t + 1)
                        high(n - 1, (s + 1) % 2)
                        if s == 2:
                            x1_high(t + 1)
                        if s == 3:
                            exps(t + 1)
                        if s == 4:
                            onehots_out(t + 1)

            @block.vector
            def _(dve):
                nc.vector.memset(simb[:], 0.0).then_inc(sim_zero, 1)
                nc.vector.memset(ones[:], 1.0).then_inc(set_up, 1)
                nc.vector.memset(half_pow[:], -0.5).then_inc(set_up, 1)
                nc.vector.memset(pace[:], 0.0).then_inc(y_free, 1)
                nc.vector.memset(ob[:], 0.0).then_inc(out_stored, 16)
                dve.wait_ge(consts, 16 * 9)
                nc.vector.tensor_copy(wo[0][:], wo_f[:]).then_inc(set_up, 1)
                nc.vector.tensor_copy(gate[0][:], gate_f[:]).then_inc(set_up, 1)
                dve.wait_ge(set_up, 4)
                nc.vector.tensor_tensor(wo[1][:], wo_f[:], wo[0][:].bitcast(F32), ALU.subtract).then_inc(set_up, 1)
                nc.vector.tensor_tensor(gate[1][:], gate_f[:], gate[0][:].bitcast(F32), ALU.subtract).then_inc(set_up, 1)
                nc.vector.copy_predicated(simb[:], ident[:].bitcast(U32), ones[:]).then_inc(set_up, 1)
                nc.vector.memset(coef[:], 0.0).then_inc(set_up, 1)
                dve.wait_ge(set_up, SETUP)

                count = [0]
                base = [0]

                def link(ins):
                    count[0] += 1
                    ins.then_inc(chain, 1)
                    return base[0] + count[0]

                def then(value):
                    dve.wait_ge(chain, value)

                def then_plain(value):
                    dve.wait_ge(chain, value)
                    nc.vector.memset(pace[:], 0.0)

                def gated(n, r, first):
                    dve.wait_ge(tanh_done, n + 1)
                    if not first:
                        dve.wait_ge(c_done, n - 1)
                    nc.vector.scalar_tensor_tensor(hg[r][:], th[r][:], 1.0, g_ps[r][:, 0:QF], ALU.add,
                                                   ALU.mult).then_inc(a_done, 1)

                def hidden(n, r, first):
                    dve.wait_ge(c_done, n + 1)
                    dve.wait_ge(u_done, n + 1)
                    if not first:
                        dve.wait_ge(hT_done, n - 1)
                    nc.vector.tensor_tensor(hh[r][:], hc[r][:], u_ps[r][:, 0:QF], ALU.mult).then_inc(h_done, 1)

                def low(n, r):
                    dve.wait_ge(hi_done, n + 1)
                    nc.vector.tensor_tensor(hT[r][1][:], hT_ps[r][:, 0:QF], hT[r][0][:].bitcast(F32),
                                            ALU.subtract).then_inc(lo_done, 1)

                def normalise(T):
                    m = m_ps[:].rearrange("p (g h r) -> p g h r", g=GPB, h=GH)
                    dve.wait_ge(oT_done, T + 1)
                    k = link(nc.vector.reciprocal(rsum[:], m[:, :, :, HD]))
                    then(k)
                    nc.vector.tensor_tensor(attn[:].rearrange("p (g h d) -> p g h d", g=GPB, h=GH), m[:, :, :, 0:HD],
                                            rsum[:].unsqueeze(3).to_broadcast([P, GPB, GH, HD]),
                                            ALU.mult).then_inc(attn_ready, 1)

                def attn_low(T):
                    dve.wait_ge(aT_hi, T + 1)
                    nc.vector.tensor_tensor(aT[1][:].rearrange("p c n -> p (c n)"), m_ps[:, 0:D],
                                            aT[0][:].rearrange("p c n -> p (c n)").bitcast(F32),
                                            ALU.subtract).then_inc(aT_lo, 1)

                def norm(src, src_sem, value, st, m, ve, ve_sem, rs, rs_sem, turn, dst, dst_sem, before=None):
                    dve.wait_ge(src_sem, value)
                    k = link(nc.vector.bn_stats(st[:], src[:]))
                    then_plain(k)
                    k = link(nc.vector.bn_aggr(m[:], st[:]))
                    then(k)
                    nc.vector.tensor_scalar(ve[:], m[:, 1:2], EPS, None, ALU.add).then_inc(ve_sem, 1)
                    dve.wait_ge(rs_sem, turn)
                    if before is not None:
                        dve.wait_ge(*before)
                    nc.vector.tensor_scalar(dst[:], src[:], m[:, 0:1], rs[:], ALU.subtract, ALU.mult).then_inc(dst_sem, 1)

                def first_norm(T):
                    dve.wait_ge(wo_done, T + 1)
                    dve.wait_ge(xt_loaded, T * 16 + 16)
                    nc.vector.tensor_tensor(z[:], m_ps[:, 0:D], xt[:], ALU.add).then_inc(z_done, 1)
                    norm(z, z_done, T + 1, stats, mv, veps, veps_ready, rstd, rstd_ready, T + 1, x1n, x1n_ready)

                def x1_low(T):
                    dve.wait_ge(xT_hi, T + 1)
                    nc.vector.tensor_tensor(xTn[1][:].rearrange("p c n -> p (c n)"), m_ps[:, 0:D],
                                            xTn[0][:].rearrange("p c n -> p (c n)").bitcast(F32),
                                            ALU.subtract).then_inc(xT_lo, 1)

                def logits_max(T):
                    dve.wait_ge(logits_done, T + 1)
                    nc.vector.tensor_reduce(nmax[:], m_ps[:, 0:E], AX.X, ALU.max, negate=True).then_inc(nmax_ready, 1)

                def top_experts(T):
                    dve.wait_ge(ex_done, T + 1)
                    k = link(nc.vector.reciprocal(re[:], esum[:]))
                    then(k)
                    k = link(nc.vector.tensor_scalar(probs[:], ex[:], re[:], None, ALU.mult))
                    then_plain(k)
                    k = link(nc.vector.max(top[:], probs[:]))
                    then(k)
                    k = link(nc.vector.reduce_sum(wsum[:], top[:], AX.X))
                    ki = link(nc.vector.max_index(idx[:], top[:], probs[:]))
                    then(ki)
                    ki = link(nc.vector.tensor_copy(idxf[:], idx[:]))
                    k = link(nc.vector.tensor_scalar(wclip[:], wsum[:], 1e-12, None, ALU.max))
                    then(ki)
                    nc.vector.tensor_tensor(oh[:], iota[:].unsqueeze(1).to_broadcast([P, TOPK, E]),
                                            idxf[:].unsqueeze(2).to_broadcast([P, TOPK, E]),
                                            ALU.is_equal).then_inc(oh_ready, 1)
                    then(k)
                    k = link(nc.vector.reciprocal(winv[:], wclip[:]))
                    then(k)
                    link(nc.vector.tensor_scalar(w8[:], top[:], winv[:], 0.5, ALU.mult, ALU.mult))

                def nearest(T):
                    dve.wait_ge(prod_done, T + 1)
                    k = link(nc.vector.reduce_sum(cand[:], prod[:], AX.X))
                    then(k)
                    k = link(nc.vector.tensor_reduce(best[:], cand[:], AX.X, ALU.max))
                    then(k)
                    link(nc.vector.tensor_scalar(keep[:], best[:], THRESH, None, ALU.is_lt))
                    k = link(nc.vector.tensor_tensor(eq[:], cand[:], best[:].unsqueeze(2).to_broadcast([P, SEL, SEL]),
                                                     ALU.is_equal))
                    then(k)
                    link(nc.vector.tensor_tensor(coef[:, SEL:TOPK], keep[:], w8[:, SEL:TOPK], ALU.mult))
                    k = link(nc.vector.tensor_tensor(wt[:], eq[:], rankw[:].unsqueeze(1).to_broadcast([P, SEL, SEL]),
                                                     ALU.mult))
                    then(k)
                    link(nc.vector.tensor_tensor(move[:], w8[:, SEL:TOPK], coef[:, SEL:TOPK], ALU.subtract))
                    k = link(nc.vector.tensor_reduce(wm[:], wt[:], AX.X, ALU.max))
                    then(k)
                    k = link(nc.vector.tensor_tensor(sel[:], wt[:], wm[:].unsqueeze(2).to_broadcast([P, SEL, SEL]),
                                                     ALU.is_equal))
                    then(k)
                    k = link(nc.vector.tensor_tensor(moved[:], sel[:], move[:].unsqueeze(2).to_broadcast([P, SEL, SEL]),
                                                     ALU.mult))
                    then(k)
                    k = link(nc.vector.reduce_sum(added[:], moved[:].rearrange("p s q -> p q s"), AX.X))
                    then(k)
                    nc.vector.tensor_tensor(coef[:, 0:SEL], added[:], w8[:, 0:SEL], ALU.add).then_inc(coef_ready, 1)

                def combine(T, used):
                    dve.wait_ge(prod2_done, T + 1)
                    if used is not None:
                        dve.wait_ge(c_done, used)
                    nc.vector.reduce_sum(cw[:], prod2[:].rearrange("p k e -> p e k"), AX.X).then_inc(cw_ready, 1)

                for piece in (normalise, attn_low, first_norm, x1_low, logits_max, top_experts, nearest):
                    piece(0)
                combine(0, None)
                k = link(nc.vector.tensor_copy(x1[:], x1n[:]))
                then(k)
                gated(0, 0, True)
                hidden(0, 0, True)
                gated(1, 1, True)
                low(0, 0)
                hidden(1, 1, True)
                before = count[0]
                count[0] = 0
                per = CHAIN
                with dve.Fori(0, TILES) as t:
                    base[0] = t * per + before
                    for s in range(QUADS):
                        n = t * QUADS + s + 2
                        gated(n, s % 2, False)
                        if s == 1:
                            attn_low(t + 1)
                        if s == 3:
                            logits_max(t + 1)
                        low(n - 1, (s + 1) % 2)
                        hidden(n, s % 2, False)
                        if s == 0:
                            normalise(t + 1)
                        if s == 1:
                            first_norm(t + 1)
                        if s == 2:
                            x1_low(t + 1)
                        if s == 3:
                            top_experts(t + 1)
                        if s == 5:
                            nearest(t + 1)
                            combine(t + 1, t * QUADS + QUADS)
                        if s == QUADS - 1:
                            dve.wait_ge(d_done, t * QUADS + QUADS)
                            nc.vector.tensor_tensor(r2[:], y_ps[:, 0:D], x1[:], ALU.add).then_inc(y_free, 1)
                            norm(r2, y_free, t + 2, stats2, mv2, veps2, veps2_ready, rstd2, rstd2_ready, t + 1, ob,
                                 out_ready, before=(out_stored, t * 16 + 16))
                            k = link(nc.vector.tensor_copy(x1[:], x1n[:]))
                    assert count[0] == per, (count[0], before)

            @block.gpsimd
            def _(pool):
                def weighted(n, r, q, first):
                    pool.wait_ge(a_done, n + 1)
                    if not first:
                        pool.wait_ge(h_done, n - 1)
                    v = lambda tile: tile[:].rearrange("p (e f) -> p e f", f=FF)
                    nc.gpsimd.tensor_tensor(v(hc[r]), v(hg[r]),
                                            cw[:, q * QE:(q + 1) * QE].unsqueeze(2).to_broadcast([P, QE, FF]),
                                            ALU.mult).then_inc(c_done, 1)

                def power(ve, ve_sem, rs, rs_sem, value):
                    pool.wait_ge(ve_sem, value)
                    nc.gpsimd.tensor_tensor(rs[:], ve[:], half_pow[:], ALU.pow).then_inc(rs_sem, 1)

                def candidates(T):
                    pool.wait_ge(simrow_ready, T + 1)
                    nc.gpsimd.tensor_tensor(prod[:], simrow[:].unsqueeze(2).to_broadcast([P, SEL, SEL, E]),
                                            oh[:, 0:SEL, :].unsqueeze(1).to_broadcast([P, SEL, SEL, E]),
                                            ALU.mult).then_inc(prod_done, 1)

                def spread(T):
                    pool.wait_ge(coef_ready, T + 1)
                    nc.gpsimd.tensor_tensor(prod2[:], oh[:], coef[:].unsqueeze(2).to_broadcast([P, TOPK, E]),
                                            ALU.mult).then_inc(prod2_done, 1)

                pool.wait_ge(set_up, SETUP)
                power(veps, veps_ready, rstd, rstd_ready, 1)
                candidates(0)
                spread(0)
                pool.wait_ge(cw_ready, 1)
                weighted(0, 0, 0, True)
                weighted(1, 1, 1, True)
                with pool.Fori(0, TILES) as t:
                    for s in range(QUADS):
                        n = t * QUADS + s + 2
                        if s == QUADS - 2:
                            pool.wait_ge(cw_ready, t + 2)
                        weighted(n, s % 2, (s + 2) % QUADS, False)
                        if s == 1:
                            power(veps, veps_ready, rstd, rstd_ready, t + 2)
                        if s == 5:
                            candidates(t + 1)
                            spread(t + 1)
                        if s == QUADS - 1:
                            power(veps2, veps2_ready, rstd2, rstd2_ready, t + 1)


_INS = ["xT", "x", "Wq", "Wk", "Wv", "Wo", "gateT", "guT", "dT", "sim", "ident", "iota", "rankw", "maskS", "maskST"]


def laid_out(i):
    import numpy as np
    a = {k: np.asarray(v) for k, v in i.items()}
    x = np.ascontiguousarray(a["L0_attn_x"].reshape(N, D))
    gu = a["L0_ffn_gate_up_proj"].reshape(QUADS, QE, 2, FF, KC, P)
    dn = a["L0_ffn_down_proj"].transpose(0, 2, 1).reshape(QUADS, QJ, P, D)
    keys, queries = np.arange(P)[None, :], np.arange(P)[:, None]
    return {
        "xT": np.ascontiguousarray(x.reshape(N, KC, P).transpose(2, 1, 0)),
        "x": x,
        "Wq": np.ascontiguousarray(a["L0_attn_Wq"]),
        "Wk": np.ascontiguousarray(a["L0_attn_Wk"]),
        "Wv": np.ascontiguousarray(a["L0_attn_Wv"]),
        "Wo": np.ascontiguousarray(a["L0_attn_Wo"]),
        "gateT": np.ascontiguousarray(a["L0_ffn_gate_weight"].T),
        "guT": np.ascontiguousarray(gu.transpose(5, 0, 2, 4, 1, 3).reshape(P, QUADS, GUW)),
        "dT": np.ascontiguousarray(dn.transpose(2, 0, 1, 3).reshape(P, QUADS, QJ * D)),
        "sim": np.ascontiguousarray(a["L0_ffn_similarity"]),
        "ident": np.eye(P, dtype=np.float32),
        "iota": np.ascontiguousarray(np.broadcast_to(np.arange(E, dtype=np.float32), (P, E))),
        "rankw": np.ascontiguousarray(np.broadcast_to(np.arange(SEL, 0, -1, dtype=np.float32), (P, SEL))),
        "maskS": np.where(keys > queries, np.float32(NEG), np.float32(0)).astype(np.float32),
        "maskST": np.where(keys < queries, np.float32(NEG), np.float32(0)).astype(np.float32),
    }


def kernel(**inputs):
    import concourse.bacc as bacc
    from concourse.bass_utils import run_bass_kernel_spmd

    arrays = laid_out(inputs)
    nc = bacc.Bacc("TRN2", target_bir_lowering=False, num_devices=1)
    args = [nc.dram_tensor(f"in_{k}", arrays[k].shape, F32, kind="ExternalInput").ap() for k in _INS]
    out = nc.dram_tensor("out", (N, D), F32, kind="ExternalOutput").ap()
    moe_block(nc, *args, out)
    r = run_bass_kernel_spmd(nc, [{f"in_{k}": arrays[k] for k in _INS}], core_ids=[0])
    return r.results[0]["out"].reshape(B, T, D)
```

```python
from contextlib import ExitStack

import concourse.bass as bass
from concourse import mybir

F32 = mybir.dt.float32
F32R = mybir.dt.float32r
BF16 = mybir.dt.bfloat16
U32 = mybir.dt.uint32
ALU = mybir.AluOpType
ACT = mybir.ActivationFunctionType
AX = mybir.AxisListType

P = 128
B, T, D = 4, 1024, 256
H, HD = 16, 16
KC = D // P
N = B * T
TILES = N // P
CH = 512
HALVES = T // CH
GH = 4
GPB = H // GH
GROUPS = B * GPB
KB = T // P
VW = 32
PARTS = 3
Q_PART = (0, 0, 0, 1, 1, 2)
K_PART = (0, 1, 2, 0, 1, 0)
SROWS = 16 * len(Q_PART)
MROWS = SROWS + PARTS
NEG = -1.0e30
SCALE = float(HD) ** -0.5

E, FF = 32, 96
TOPK, SEL = 8, 4
THRESH = 0.5
QE = 4
QUADS = E // QE
QF = QE * FF
QJ = QF // P
GUW = 2 * KC * QF
WQ = GUW + QJ * D
STAGE = WQ // 3
PIECES = QUADS * 3
EPS = 1e-5


def steps_of_group():
    return [(c, kb) for c in range(HALVES) for kb in range(KB // HALVES * (c + 1))]


def first_col(c, kb):
    return max(0, kb - c * (CH // P)) * P


def max_units():
    units = []
    for qt in range(KB):
        for k0 in range(0, (qt + 1) * P, CH):
            keys = min((qt + 1) * P - k0, CH)
            per = CH // keys
            for h0 in range(0, GH, per):
                units.append([(h, qt, k0, keys, (h - h0) * keys) for h in range(h0, min(h0 + per, GH))])
    return units


STEPS = steps_of_group()
NS = len(STEPS)
XS = NS * GH
UNITS = max_units()
UNITS_A = [u for u in UNITS if u[0][1] < KB // 2]
TURN_B = 1
A_LAG = 3
TURN_A = len(UNITS_A) + A_LAG + 1
RING = len(UNITS) + 2
BANKS = 3


def ring_bank(u):
    return (TURN_B + 1 if u == TURN_B else u - (u > TURN_B)) % BANKS


def ring_before(u, first):
    if u == TURN_B:
        return TURN_B - 2
    if u == TURN_B + 2 and not first:
        return TURN_B
    return u - BANKS - (TURN_B < u <= TURN_B + BANKS)


def ring_uses(G, u):
    if isinstance(G, int) and G == 0:
        return u - (u > TURN_B)
    return G * RING - 1 + u


def unit_of(u):
    return UNITS[u - (u > TURN_B) - (u > TURN_A)]


def ring_share():
    width = [CH - first_col(c, kb) for c, kb in STEPS]
    spent, marks = 0.0, {}
    for s in range(NS):
        for h in range(GH):
            spent += width[s] + P
            if h == GH - 1:
                spent += 4 * width[s - 1]
            marks[s, h] = spent
    return {k: round(RING * v / spent) for k, v in marks.items()}


def moe_block(
    nc, xT, x, Wq, Wk, Wv, Wo, gateT, guT, dT, sim, ident, iota, rankw, maskS, maskST, out,
):
    with ExitStack() as ctx:
        q_dram = nc.dram_tensor("q_parts", (PARTS, B, HALVES, GPB, HD, GH, CH), BF16, kind="Internal").ap()
        k_dram = nc.dram_tensor("k_stack", (B, SROWS, T), BF16, kind="Internal").ap()
        v_dram = nc.dram_tensor("v_ones", (B, P, KB, VW), F32, kind="Internal").ap()
        o_dram = nc.dram_tensor("o_sums", (TILES, P, GPB, P), F32, kind="Internal").ap()
        project(nc, xT, Wq, Wk, Wv, ident, q_dram, k_dram, v_dram)
        w_hi = ctx.enter_context(nc.sbuf_tensor("w_hi", [P, QUADS * WQ], F32R))
        w_lo = ctx.enter_context(nc.sbuf_tensor("w_lo", [P, QUADS * WQ], F32R))
        attend(nc, q_dram, k_dram, v_dram, o_dram, guT, dT, w_hi, w_lo, ident, maskS, maskST)
        experts(nc, o_dram, x, Wo, gateT, sim, ident, iota, rankw, w_hi, w_lo, out)


def project(nc, xT, Wq, Wk, Wv, ident_d, q_dram, k_dram, v_dram):
    with ExitStack() as ctx:
        sb = lambda name, shape, dt: ctx.enter_context(nc.sbuf_tensor(name, shape, dt))
        ps = lambda name, shape: ctx.enter_context(nc.psum_tensor(name, shape, F32))
        sem = lambda name: ctx.enter_context(nc.semaphore(name))
        wq = sb("a_wq", [P, KC, D], F32)
        wkv = sb("a_wkv", [P, KC, 2 * HD], F32)
        ident = sb("a_ident", [P, P], F32)
        kvT = [sb(f"a_kvT{s}", [P, CH], F32) for s in range(2)]
        xt = [sb(f"a_xt{s}", [P, KC, CH], F32) for s in range(2)]
        parts = [sb(f"a_parts{s}", [P, 3, PARTS, CH], BF16) for s in range(2)]
        rest = [sb(f"a_rest{s}", [P, 3, CH], F32) for s in range(2)]
        vt = [sb(f"a_vt{s}", [P, CH // P, VW], F32) for s in range(2)]
        qk_ps = [[ps(f"a_ps{s}{j}", [P, CH]) for j in range(3)] for s in range(2)]
        v_ps = [ps(f"a_psv{s}", [P, CH]) for s in range(2)]
        w_loaded = sem("a_w_loaded")
        xt_loaded = [sem(f"a_xt_loaded{s}") for s in range(2)]
        mm_done = sem("a_mm_done")
        kvT_ready = sem("a_kvT_ready")
        v_done = sem("a_v_done")
        p1_done = sem("a_p1_done")
        rest_done = sem("a_rest_done")
        p2_done = sem("a_p2_done")
        p3_done = sem("a_p3_done")
        vt_ready = sem("a_vt_ready")
        vt_set = sem("a_vt_set")
        stored = [sem(f"a_stored{s}") for s in range(2)]
        STORES = 16 * (2 + PARTS + 1)
        rows = lambda j: P if j < 2 else HD

        with nc.Block() as block:

            @block.sync
            def _(sp):
                sp.dma_start(wq[:], Wq.rearrange("(c p) n -> p c n", p=P)).then_inc(w_loaded, 16)
                sp.dma_start(wkv[:, :, 0:HD], Wk.rearrange("(c p) n -> p c n", p=P)).then_inc(w_loaded, 16)
                sp.dma_start(wkv[:, :, HD:], Wv.rearrange("(c p) n -> p c n", p=P)).then_inc(w_loaded, 16)
                for s in range(2):
                    sp.dma_start(xt[s][:], xT[:, :, s * CH:(s + 1) * CH]).then_inc(xt_loaded[s], 16)
                sp.dma_start(ident[:], ident_d).then_inc(w_loaded, 16)

                def chunk(b, s, more):
                    n = b * 2 + s
                    if more:
                        sp.wait_ge(mm_done, n * 3 + 3)
                        sp.dma_start(xt[s][:], xT[:, :, bass.ds(n * CH + 2 * CH, CH)]).then_inc(xt_loaded[s], 16)
                    sp.wait_ge(p2_done, n * 3 + 3)
                    sp.wait_ge(p3_done, n * 3 + 3)
                    for j in range(2):
                        dst = q_dram[:, bass.ds(b, 1), s, 2 * j:2 * j + 2]
                        sp.dma_start(dst.rearrange("c o g d h t -> (o g d h) c t"), parts[s][:, j]).then_inc(stored[s], 16)
                    for blk, copies in ((0, 3), (3, 2), (5, 1)):
                        dst = k_dram[bass.ds(b, 1), HD * blk:HD * (blk + copies), s * CH:(s + 1) * CH]
                        sp.dma_start(dst.rearrange("o (c d) t -> (o d) c t", d=HD),
                                     parts[s][0:HD, 2, 0:copies, :]).then_inc(stored[s], 16)
                    sp.wait_ge(vt_ready, n + 1)
                    tiles = CH // P
                    sp.dma_start(v_dram[bass.ds(b, 1), :, s * tiles:(s + 1) * tiles].rearrange("o p k w -> (o p) k w"),
                                 vt[s][:]).then_inc(stored[s], 16)

                with sp.Fori(0, B - 1) as b:
                    for s in range(2):
                        chunk(b, s, True)
                for s in range(2):
                    chunk(B - 1, s, False)
                for s in range(2):
                    sp.wait_ge(stored[s], B * STORES)

            @block.tensor
            def _(pe):
                pe.wait_ge(w_loaded, 64)

                def chunk(b, s, reused):
                    n = b * 2 + s
                    pe.wait_ge(xt_loaded[s], b * 16 + 16)
                    for j in (2, 0, 1):
                        if reused and j == 2:
                            pe.wait_ge(kvT_ready, n - 1)
                        elif reused:
                            pe.wait_ge(rest_done, n * 3 - 6 + 2 + j)
                        w = wkv[:] if j == 2 else wq[:, :, j * P:(j + 1) * P]
                        m = 2 * HD if j == 2 else P
                        for c in range(KC):
                            last = nc.tensor.matmul(qk_ps[s][j][0:m, :], w[:, c, :], xt[s][:, c, :],
                                                    start=(c == 0), stop=(c == KC - 1))
                        last.then_inc(mm_done, 1)
                    pe.wait_ge(kvT_ready, n + 1)
                    if reused:
                        pe.wait_ge(vt_ready, n - 1)
                    for k in range(CH // P):
                        last = nc.tensor.transpose(v_ps[s][:, k * P:(k + 1) * P], kvT[s][:, k * P:(k + 1) * P], ident[:])
                    last.then_inc(v_done, 1)

                for s in range(2):
                    chunk(0, s, False)
                with pe.Fori(1, B) as b:
                    for s in range(2):
                        chunk(b, s, True)

            @block.scalar
            def _(act):
                act.wait_ge(vt_set, 2)

                def chunk(b, s, reused):
                    n = b * 2 + s
                    act.wait_ge(mm_done, n * 3 + 1)
                    if reused:
                        act.wait_ge(v_done, n - 1)
                        act.wait_ge(rest_done, n * 3 - 5)
                    nc.scalar.copy(kvT[s][0:2 * HD, :], qk_ps[s][2][0:2 * HD, :]).then_inc(kvT_ready, 1)
                    act.wait_ge(kvT_ready, n + 1)
                    if reused:
                        act.wait_ge(stored[s], b * STORES)
                    nc.scalar.copy(parts[s][0:HD, 2, 0, :], kvT[s][0:HD, :]).then_inc(p1_done, 1)
                    for j in range(2):
                        act.wait_ge(mm_done, n * 3 + j + 2)
                        nc.scalar.copy(parts[s][:, j, 0, :], qk_ps[s][j][:]).then_inc(p1_done, 1)
                    for i, j in enumerate((2, 0, 1)):
                        act.wait_ge(rest_done, n * 3 + i + 1)
                        nc.scalar.copy(parts[s][0:rows(j), j, 1, :], rest[s][0:rows(j), j, :]).then_inc(p2_done, 1)

                for s in range(2):
                    chunk(0, s, False)
                with act.Fori(1, B) as b:
                    for s in range(2):
                        chunk(b, s, True)

            @block.vector
            def _(dve):
                for s in range(2):
                    nc.vector.memset(vt[s][:, :, HD + 1:VW], 0.0)
                    nc.vector.memset(vt[s][:, :, HD:HD + 1], 1.0)
                    nc.vector.memset(kvT[s][:], 0.0).then_inc(vt_set, 1)

                def chunk(b, s, reused):
                    n = b * 2 + s
                    for i, j in enumerate((2, 0, 1)):
                        if reused:
                            dve.wait_ge(p3_done, n * 3 - 6 + i + 1)
                        dve.wait_ge(p1_done, n * 3 + i + 1)
                        src = kvT[s] if j == 2 else qk_ps[s][j]
                        nc.vector.tensor_tensor(rest[s][0:rows(j), j, :], src[0:rows(j), :],
                                                parts[s][0:rows(j), j, 0, :], ALU.subtract).then_inc(rest_done, 1)
                    if reused:
                        dve.wait_ge(stored[s], b * STORES)
                    dve.wait_ge(v_done, n + 1)
                    nc.vector.tensor_copy(vt[s][:, :, 0:HD], v_ps[s][:].rearrange(
                        "p (k d) -> p k d", d=P)[:, :, HD:2 * HD]).then_inc(vt_ready, 1)

                for s in range(2):
                    chunk(0, s, False)
                with dve.Fori(1, B) as b:
                    for s in range(2):
                        chunk(b, s, True)

            @block.gpsimd
            def _(pool):
                with pool.Fori(0, B) as b:
                    for s in range(2):
                        n = b * 2 + s
                        for i, j in enumerate((2, 0, 1)):
                            pool.wait_ge(p2_done, n * 3 + i + 1)
                            nc.gpsimd.tensor_tensor(parts[s][0:rows(j), j, 2, :], rest[s][0:rows(j), j, :],
                                                    parts[s][0:rows(j), j, 1, :], ALU.subtract).then_inc(p3_done, 1)


def attend(nc, q_dram, k_dram, v_dram, o_dram, guT, dT, w_hi, w_lo, ident_d, maskS_d, maskST_d):
    with ExitStack() as ctx:
        sb = lambda name, shape, dt: ctx.enter_context(nc.sbuf_tensor(name, shape, dt))
        ps = lambda name, shape: ctx.enter_context(nc.psum_tensor(name, shape, F32))
        sem = lambda name: ctx.enter_context(nc.semaphore(name))
        qs = [sb(f"b_qs{r}", [P, HALVES, GH, CH], BF16) for r in range(2)]
        km = [sb(f"b_km{r}", [P, T], BF16) for r in range(2)]
        ks = [sb(f"b_ks{r}", [P, T], BF16) for r in range(2)]
        vs = [sb(f"b_vs{r}", [P, KB, VW], F32) for r in range(2)]
        pr = [sb(f"b_pr{r}", [P, GH, CH], F32) for r in range(2)]
        osb = [sb(f"b_osb{c}", [P, CH], F32) for c in range(HALVES)]
        stage = [sb(f"b_stage{r}", [P, STAGE], F32) for r in range(2)]
        ident = sb("b_ident", [P, P], F32)
        masks = sb("b_masks", [P, 2, P], F32)
        identb = sb("b_identb", [P, P], BF16)
        maskS = sb("b_maskS", [P, P], BF16)
        maskST = sb("b_maskST", [P, P], BF16)
        mx = sb("b_mx", [P, 2, GH, GH], F32)
        mx2 = sb("b_mx2", [P, GH, GH], F32)
        mrow = sb("b_mrow", [16, 2, PARTS, P], BF16)
        mrest = sb("b_mrest", [16, 2, 2, P], F32)
        st_ps = [ps(f"b_st{r}", [P, CH]) for r in range(BANKS)]
        pv_ps = [ps(f"b_pv{c}", [P, CH]) for c in range(HALVES)]
        ring_ps = [ps(f"b_ring{r}", [P, CH]) for r in range(BANKS)]

        consts = sem("b_consts")
        masks_ready = sem("b_masks_ready")
        a_loaded = [sem(f"b_a_loaded{r}") for r in range(2)]
        b_loaded = [sem(f"b_b_loaded{r}") for r in range(2)]
        LOADS_A, LOADS_B = 16 * (PARTS + 1), 16 * (PARTS + 2)
        st_ready = sem("b_st_ready")
        exp_done = sem("b_exp_done")
        pv_done = sem("b_pv_done")
        o_copied = sem("b_o_copied")
        o_stored = [sem(f"b_o_stored{c}") for c in range(HALVES)]
        ring_ready = sem("b_ring_ready")
        ring_free = sem("b_ring_free")
        mx_ready = sem("b_mx_ready")
        vec_chain = sem("b_vec_chain")
        mrow_ready = sem("b_mrow_ready")
        m_loaded = [sem(f"b_m_loaded{h}") for h in range(2)]
        staged = [sem(f"b_staged{r}") for r in range(2)]
        cut = sem("b_cut")
        share = ring_share()

        def over_groups(eng, first, both, last):
            first(0, 0)
            with eng.Fori(0, GROUPS // 2 - 1) as i:
                both(i * 2 + 1, 1)
                both(i * 2 + 2, 0)
            last(GROUPS - 1, 1)

        with nc.Block() as block:

            @block.sync
            def _(sp):
                def load_q(G, r, c, done):
                    at = 0
                    for part in range(PARTS):
                        copies = Q_PART.count(part)
                        src = q_dram[part, bass.ds(G // GPB, 1), c, bass.ds(G % GPB, 1)].rearrange(
                            "o g d h t -> (o g) d (h t)")
                        sp.dma_start(qs[r][at:at + HD * copies, c].rearrange("d h t -> d (h t)"),
                                     src.to_broadcast([copies, HD, GH * CH])).then_inc(done, 16)
                        at += HD * copies

                def load_a(G, r, before):
                    if before is not None:
                        sp.wait_ge(ring_ready, ring_uses(before, RING))
                        sp.wait_ge(st_ready, before * XS + KB // HALVES * GH)
                    load_q(G, r, 0, a_loaded[r])
                    sp.dma_start(km[r][0:SROWS, :], k_dram[bass.ds(G // GPB, 1)].rearrange("o d t -> (o d) t")).then_inc(a_loaded[r], 16)

                def load_b(G, r, before):
                    if before is not None:
                        sp.wait_ge(pv_done, before * NS + NS)
                    load_q(G, r, 1, b_loaded[r])
                    sp.dma_start(ks[r][0:SROWS, :], k_dram[bass.ds(G // GPB, 1)].rearrange("o d t -> (o d) t")).then_inc(b_loaded[r], 16)
                    sp.dma_start(vs[r][:], v_dram[bass.ds(G // GPB, 1)].rearrange("o p k w -> (o p) k w")).then_inc(b_loaded[r], 16)

                def m_rows(G, r, half):
                    sp.wait_ge(mrow_ready, G * 2 + half + 1)
                    for c in range(PARTS):
                        sp.dma_start(qs[r][SROWS + c:SROWS + c + 1, half], mrow[:, half, c, :]).then_inc(m_loaded[half], 16)

                def store(G, c):
                    sp.wait_ge(o_copied, G * HALVES + c + 1)
                    tiles = CH // P
                    dst = o_dram[bass.ds((G // GPB) * KB + c * tiles, tiles), :, bass.ds(G % GPB, 1)]
                    sp.dma_start(dst.rearrange("t r o x -> r (t o) x"),
                                 osb[c][:].rearrange("r (t x) -> r t x", x=P)).then_inc(o_stored[c], 16)

                sp.dma_start(ident[:], ident_d).then_inc(consts, 16)
                sp.dma_start(masks[:, 0], maskS_d).then_inc(consts, 16)
                sp.dma_start(masks[:, 1], maskST_d).then_inc(consts, 16)
                for G in range(2):
                    load_a(G, G, None)
                    load_b(G, G, None)
                m_rows(0, 0, 0)
                m_rows(0, 0, 1)
                load_a(2, 0, 0)
                m_rows(1, 1, 0)
                store(0, 0)

                def group(G, r, more_a=True):
                    load_b(G + 1, 1 - r, G - 1)
                    m_rows(G, r, 1)
                    store(G - 1, 1)
                    if more_a:
                        load_a(G + 2, r, G)
                    m_rows(G + 1, 1 - r, 0)
                    store(G, 0)

                m_rows(1, 1, 1)
                store(0, 1)
                load_b(2, 0, 0)
                load_a(3, 1, 1)
                m_rows(2, 0, 0)
                store(1, 0)
                with sp.Fori(1, GROUPS // 2 - 1) as i:
                    group(i * 2, 0)
                    group(i * 2 + 1, 1)
                group(GROUPS - 2, 0, more_a=False)
                m_rows(GROUPS - 1, 1, 1)
                store(GROUPS - 2, 1)
                store(GROUPS - 1, 0)
                store(GROUPS - 1, 1)
                for c in range(HALVES):
                    sp.wait_ge(o_stored[c], 16 * GROUPS)

            @block.tensor
            def _(pe):
                pe.wait_ge(masks_ready, 5)

                def turn_maxima(bank, half):
                    nc.tensor.transpose(bank[0:16, 0:P], mx[:, half].rearrange("p h q -> p (h q)"),
                                        ident[:]).then_inc(ring_ready, 1)

                def ring_unit(G, r, u):
                    bank = ring_ps[ring_bank(u)]
                    first = isinstance(G, int) and G == 0
                    before = ring_before(u, first)
                    if not (first and before < 0):
                        pe.wait_ge(ring_free, ring_uses(G, before) + 1)
                    if u == TURN_B:
                        pe.wait_ge(mx_ready, G)
                        turn_maxima(bank, 1)
                        return
                    if u == TURN_A:
                        pe.wait_ge(ring_free, ring_uses(G, len(UNITS_A) + 1))
                        turn_maxima(bank, 0)
                        return
                    if u == len(UNITS_A) + 1:
                        pe.wait_ge(b_loaded[r], (G // 2 + 1) * LOADS_B)
                    for h, qt, k0, keys, col in unit_of(u):
                        c, q0 = divmod(qt * P, CH)
                        diag = k0 + keys == (qt + 1) * P
                        last = nc.tensor.matmul(bank[:, col:col + keys], qs[r][0:SROWS, c, h, q0:q0 + P],
                                                km[r][0:SROWS, k0:k0 + keys], start=True, stop=not diag)
                        if diag:
                            last = nc.tensor.matmul(bank[:, col + keys - P:col + keys], identb[:], maskS[:],
                                                    start=False, stop=True)
                    last.then_inc(ring_ready, 1)

                def scores(G, r, s, h):
                    c, kb = STEPS[s]
                    o = first_col(c, kb)
                    x = s * GH + h
                    bank = st_ps[x % BANKS]
                    if not (isinstance(G, int) and G == 0 and x < BANKS):
                        pe.wait_ge(exp_done, G * XS + x - BANKS + 1)
                    if s == 0 and h == 0:
                        pe.wait_ge(b_loaded[r], (G // 2 + 1) * LOADS_B)
                    if kb == 0 and h == 0:
                        pe.wait_ge(m_loaded[c], (G + 1) * 16 * PARTS)
                    own = kb >= c * (CH // P)
                    last = nc.tensor.matmul(bank[:, o:CH], ks[r][0:MROWS, kb * P:(kb + 1) * P],
                                            qs[r][0:MROWS, c, h, o:CH], start=True, stop=not own)
                    if own:
                        last = nc.tensor.matmul(bank[:, o:o + P], identb[:], maskST[:], start=False, stop=True)
                    last.then_inc(st_ready, 1)

                def values(G, r, s):
                    c, kb = STEPS[s]
                    o = first_col(c, kb)
                    pe.wait_ge(exp_done, G * XS + s * GH + GH)
                    if kb == 0 and not (isinstance(G, int) and G == 0):
                        pe.wait_ge(o_copied, G * HALVES + c - 1)
                    for h in range(GH):
                        last = nc.tensor.matmul(pv_ps[c][VW * h:VW * h + VW, o:CH], vs[r][:, kb, :],
                                                pr[s % 2][:, h, o:CH], start=(kb == 0),
                                                stop=(s == NS - 1 or STEPS[s + 1][0] != c))
                    last.then_inc(pv_done, 1)

                def group(G, r, more, fresh=False):
                    nxt, u = 1 - r, 0
                    if more:
                        pe.wait_ge(a_loaded[nxt], ((G + 1) // 2 + 1) * LOADS_A)
                    for s in range(NS):
                        for h in range(GH):
                            scores(G, r, s, h)
                            if h == GH - 1:
                                if s >= 1:
                                    values(G, r, s - 1)
                                elif not fresh:
                                    values(G - 1, nxt, NS - 1)
                            if not more and (s, h) == (0, GH - 1):
                                pe.wait_ge(mx_ready, G + 1)
                                turn_maxima(ring_ps[0], 1)
                            while more and u < share[s, h]:
                                ring_unit(G + 1, nxt, u)
                                u += 1

                pe.wait_ge(a_loaded[0], LOADS_A)
                for u in range(RING):
                    if u != TURN_B:
                        ring_unit(0, 0, u)
                over_groups(pe, lambda G, r: group(G, r, True, fresh=True), lambda G, r: group(G, r, True),
                            lambda G, r: group(G, r, False))
                values(GROUPS - 1, 1, NS - 1)

            @block.scalar
            def _(act):
                def group(G, r, fresh):
                    for s, (c, kb) in enumerate(STEPS):
                        o = first_col(c, kb)
                        for h in range(GH):
                            if h == 0 and not (fresh and s < 2):
                                act.wait_ge(pv_done, G * NS + s - 1)
                            x = s * GH + h
                            act.wait_ge(st_ready, G * XS + x + 1)
                            nc.scalar.activation(pr[s % 2][:, h, o:CH], st_ps[x % BANKS][:, o:CH],
                                                 ACT.Exp, scale=SCALE).then_inc(exp_done, 1)
                        if s == KB // HALVES + 1:
                            copy_out(G, 0, fresh)
                        if s == 1 and not fresh:
                            copy_out(G - 1, 1, False)

                def copy_out(G, c, fresh):
                    if not fresh:
                        act.wait_ge(o_stored[c], G * 16)
                    act.wait_ge(pv_done, G * NS + (KB // HALVES if c == 0 else NS))
                    nc.scalar.copy(osb[c][:], pv_ps[c][:]).then_inc(o_copied, 1)

                over_groups(act, lambda G, r: group(G, r, True), lambda G, r: group(G, r, False),
                            lambda G, r: group(G, r, False))
                copy_out(GROUPS - 1, 1, False)

            @block.vector
            def _(dve):
                dve.wait_ge(consts, 48)
                nc.vector.tensor_copy(identb[:], ident[:]).then_inc(masks_ready, 1)
                nc.vector.tensor_copy(maskS[:], masks[:, 0]).then_inc(masks_ready, 1)
                nc.vector.tensor_copy(maskST[:], masks[:, 1]).then_inc(masks_ready, 1)
                for r in range(2):
                    nc.vector.memset(ks[r][SROWS:MROWS, :], 1.0).then_inc(masks_ready, 1)

                def cut_maxima(G, half, bank, uses):
                    chain = G * 4 + half * 2
                    dve.wait_ge(ring_ready, uses + 1)
                    if not (isinstance(G, int) and G == 0):
                        dve.wait_ge(m_loaded[half], G * 16 * PARTS)
                    neg, rest = mrow[:, half, 0, :], mrest[:, half, 0, :]
                    nc.vector.tensor_scalar(neg, bank[0:16, 0:P], -1.0, None, ALU.mult).then_inc(vec_chain, 1)
                    dve.wait_ge(vec_chain, chain + 1)
                    nc.vector.scalar_tensor_tensor(rest, bank[0:16, 0:P], -1.0, neg, ALU.mult,
                                                   ALU.subtract).then_inc(ring_free, 1)
                    dve.wait_ge(ring_free, uses + 1)
                    nc.vector.tensor_copy(mrow[:, half, 1, :], rest).then_inc(vec_chain, 1)
                    dve.wait_ge(vec_chain, chain + 2)
                    nc.vector.tensor_tensor(mrow[:, half, 2, :], rest, mrow[:, half, 1, :],
                                            ALU.subtract).then_inc(mrow_ready, 1)

                def ring_unit(G, u):
                    bank = ring_ps[ring_bank(u)]
                    if u == TURN_B:
                        cut_maxima(G - 1, 1, bank, ring_uses(G, u))
                        return
                    if u == TURN_A:
                        cut_maxima(G, 0, bank, ring_uses(G, u))
                        return
                    unit = unit_of(u)
                    h0, qt, k0, keys, _ = unit[0]
                    n = len(unit)
                    half, q = divmod(qt, KB // 2)
                    dst = mx2[:, h0:h0 + n, q] if k0 else mx[:, half, h0:h0 + n, q]
                    dve.wait_ge(ring_ready, ring_uses(G, u) + 1)
                    nc.vector.tensor_reduce(dst, bank[:, 0:n * keys].rearrange("p (n k) -> p n k", k=keys),
                                            AX.X, ALU.max).then_inc(ring_free, 1)

                def maxima(G, first=False):
                    for u in range(RING):
                        if not (first and u == TURN_B):
                            ring_unit(G, u)
                    dve.wait_ge(ring_free, ring_uses(G, RING))
                    nc.vector.tensor_tensor(mx[:, 1], mx[:, 1], mx2[:], ALU.max).then_inc(mx_ready, 1)

                maxima(0, True)
                over_groups(dve, lambda G, r: maxima(G + 1), lambda G, r: maxima(G + 1),
                            lambda G, r: cut_maxima(G, 1, ring_ps[0], ring_uses(G + 1, 0)))

            @block.gpsimd
            def _(pool):

                def fetch(j, r):
                    q, part = divmod(j, 3)
                    if part < 2:
                        src = guT[:, q, part * STAGE:(part + 1) * STAGE]
                    else:
                        src = dT[:, q, :]
                    pool.dma_start(stage[r][:], src).then_inc(staged[r], 16)

                fetch(0, 0)
                fetch(1, 1)
                for j in range(PIECES):
                    r = j % 2
                    at = slice(j * STAGE, (j + 1) * STAGE)
                    pool.wait_ge(staged[r], 16 * (j // 2 + 1))
                    nc.gpsimd.tensor_copy(w_hi[:, at], stage[r][:]).then_inc(cut, 1)
                    pool.wait_ge(cut, 2 * j + 1)
                    nc.gpsimd.tensor_tensor(w_lo[:, at], stage[r][:], w_hi[:, at].bitcast(F32),
                                            ALU.subtract).then_inc(cut, 1)
                    if j + 2 < PIECES:
                        pool.wait_ge(cut, 2 * j + 2)
                        fetch(j + 2, r)
                pool.wait_ge(cut, 2 * PIECES)


def experts(nc, o_dram, x_d, Wo, gateT, sim, ident_d, iota_d, rankw_d, w_hi, w_lo, out_d):
    with ExitStack() as ctx:
        sb = lambda name, shape, dt=F32: ctx.enter_context(nc.sbuf_tensor(name, shape, dt))
        ps = lambda name: ctx.enter_context(nc.psum_tensor(name, [P, CH], F32))
        sem = lambda name: ctx.enter_context(nc.semaphore(name))
        ident = sb("c_ident", [P, P])
        iota = sb("c_iota", [P, E])
        rankw = sb("c_rankw", [P, SEL])
        half_pow = sb("c_half_pow", [P, 1])
        ones = sb("c_ones", [P, P])
        wo_f = sb("c_wo_f", [P, KC, D])
        wo = [sb(f"c_wo{i}", [P, KC, D], F32R) for i in range(2)]
        gate_f = sb("c_gate_f", [P, KC, E])
        gate = [sb(f"c_gate{i}", [P, KC, E], F32R) for i in range(2)]
        simb = sb("c_simb", [P, P])
        ot = sb("c_ot", [P, GPB, P])
        xt = sb("c_xt", [P, D])
        pace = sb("c_pace", [P, 1])
        rsum = sb("c_rsum", [P, GPB, GH])
        attn = sb("c_attn", [P, D])
        aT = [sb(f"c_aT{i}", [P, KC, P], F32R) for i in range(2)]
        z = sb("c_z", [P, D])
        stats, mv, veps, rstd = sb("c_stats", [P, 6]), sb("c_mv", [P, 2]), sb("c_veps", [P, 1]), sb("c_rstd", [P, 1])
        x1n = sb("c_x1n", [P, D])
        xTn = [sb(f"c_xTn{i}", [P, KC, P], F32R) for i in range(2)]
        nmax, esum, re = sb("c_nmax", [P, 1]), sb("c_esum", [P, 1]), sb("c_re", [P, 1])
        ex, probs = sb("c_ex", [P, E]), sb("c_probs", [P, E])
        top, idx, idxf = sb("c_top", [P, TOPK]), sb("c_idx", [P, TOPK], U32), sb("c_idxf", [P, TOPK])
        wsum, wclip, winv, w8 = sb("c_wsum", [P, 1]), sb("c_wclip", [P, 1]), sb("c_winv", [P, 1]), sb("c_w8", [P, TOPK])
        oh = sb("c_oh", [P, TOPK, E])
        ohT = sb("c_ohT", [P, P])
        simrow = sb("c_simrow", [P, SEL, E])
        prod = sb("c_prod", [P, SEL, SEL, E])
        cand = sb("c_cand", [P, SEL, SEL])
        best, keep = sb("c_best", [P, SEL]), sb("c_keep", [P, SEL])
        eq, wt, wm, sel = sb("c_eq", [P, SEL, SEL]), sb("c_wt", [P, SEL, SEL]), sb("c_wm", [P, SEL]), sb("c_sel", [P, SEL, SEL])
        move, moved, added = sb("c_move", [P, SEL]), sb("c_moved", [P, SEL, SEL]), sb("c_added", [P, SEL])
        coef = sb("c_coef", [P, TOPK])
        prod2 = sb("c_prod2", [P, TOPK, E])
        x1 = sb("c_x1", [P, D])
        xT = [sb(f"c_xT{i}", [P, KC, P], F32R) for i in range(2)]
        cw = sb("c_cw", [P, E])
        th = [sb(f"c_th{r}", [P, QF]) for r in range(2)]
        hg = [sb(f"c_hg{r}", [P, QF]) for r in range(2)]
        hc = [sb(f"c_hc{r}", [P, QF]) for r in range(2)]
        hh = [sb(f"c_hh{r}", [P, QF]) for r in range(2)]
        hT = [[sb(f"c_hT{r}{i}", [P, QF], F32R) for i in range(2)] for r in range(2)]
        r2 = sb("c_r2", [P, D])
        stats2, mv2, veps2, rstd2 = sb("c_stats2", [P, 6]), sb("c_mv2", [P, 2]), sb("c_veps2", [P, 1]), sb("c_rstd2", [P, 1])
        ob = sb("c_ob", [P, D])
        g_ps = [ps(f"c_g{r}") for r in range(2)]
        u_ps = [ps(f"c_u{r}") for r in range(2)]
        hT_ps = [ps(f"c_hTp{r}") for r in range(2)]
        y_ps, m_ps = ps("c_y"), ps("c_m")

        consts = sem("c_consts")
        sim_zero = sem("c_sim_zero")
        set_up = sem("c_set_up")
        SETUP = 8
        CHAIN = 26
        g_done, u_done = sem("c_g_done"), sem("c_u_done")
        tanh_done = sem("c_tanh_done")
        a_done = sem("c_a_done")
        c_done = sem("c_c_done")
        h_done = sem("c_h_done")
        hT_done = sem("c_hT_done")
        hi_done, lo_done = sem("c_hi_done"), sem("c_lo_done")
        d_done = sem("c_d_done")
        ot_loaded, xt_loaded = sem("c_ot_loaded"), sem("c_xt_loaded")
        oT_done = sem("c_oT_done")
        attn_ready = sem("c_attn_ready")
        aT_done = sem("c_aT_done")
        aT_hi, aT_lo = sem("c_aT_hi"), sem("c_aT_lo")
        wo_done = sem("c_wo_done")
        z_done = sem("c_z_done")
        veps_ready, rstd_ready = sem("c_veps_ready"), sem("c_rstd_ready")
        x1n_ready = sem("c_x1n_ready")
        xT_done = sem("c_xT_done")
        xT_hi, xT_lo = sem("c_xT_hi"), sem("c_xT_lo")
        logits_done = sem("c_logits_done")
        nmax_ready, ex_done = sem("c_nmax_ready"), sem("c_ex_done")
        oh_ready = sem("c_oh_ready")
        ohT_done, ohT_ready = sem("c_ohT_done"), sem("c_ohT_ready")
        sim_done, simrow_ready = sem("c_sim_done"), sem("c_simrow_ready")
        prod_done = sem("c_prod_done")
        coef_ready = sem("c_coef_ready")
        prod2_done = sem("c_prod2_done")
        cw_ready = sem("c_cw_ready")
        rotated = sem("c_rotated")
        y_free = sem("c_y_free")
        veps2_ready, rstd2_ready = sem("c_veps2_ready"), sem("c_rstd2_ready")
        out_ready = sem("c_out_ready")
        out_stored = sem("c_out_stored")
        chain = sem("c_chain")

        def gu_cols(q, gu, c):
            at = q * WQ + (gu * KC + c) * QF
            return slice(at, at + QF)

        def d_cols(q, j):
            at = q * WQ + GUW + j * D
            return slice(at, at + D)

        with nc.Block() as block:

            @block.sync
            def _(sp):
                sp.wait_ge(sim_zero, 1)
                for s in range(SEL):
                    sp.dma_start(simb[E * s:E * s + E, E * s:E * s + E], sim).then_inc(consts, 16)
                for dst, src in ((ident, ident_d), (iota, iota_d), (rankw, rankw_d)):
                    sp.dma_start(dst[:], src).then_inc(consts, 16)
                sp.dma_start(wo_f[:], Wo.rearrange("(c p) n -> p c n", p=P)).then_inc(consts, 16)
                sp.dma_start(gate_f[:], gateT.rearrange("(c p) n -> p c n", p=P)).then_inc(consts, 16)

                def load_o(T):
                    sp.dma_start(ot[:], o_dram[bass.ds(T, 1)].rearrange("o p g x -> (o p) g x")).then_inc(ot_loaded, 16)

                def load_x(T):
                    sp.dma_start(xt[:], x_d[bass.ds(T * P, P), :]).then_inc(xt_loaded, 16)

                load_o(0)
                load_x(0)
                sp.wait_ge(oT_done, 1)
                load_o(1)
                sp.wait_ge(z_done, 1)
                load_x(1)
                with sp.Fori(0, TILES) as t:
                    nxt = (t + 2) % TILES
                    sp.wait_ge(oT_done, t + 2)
                    load_o(nxt)
                    sp.wait_ge(z_done, t + 2)
                    load_x(nxt)
                    sp.wait_ge(out_ready, t + 1)
                    sp.dma_start(out_d[bass.ds(t * P, P), :], ob[:]).then_inc(out_stored, 16)
                sp.wait_ge(ot_loaded, 16 * (TILES + 2))
                sp.wait_ge(xt_loaded, 16 * (TILES + 2))
                sp.wait_ge(out_stored, 16 * (TILES + 1))

            @block.tensor
            def _(pe):
                def passes(dst, lhs, rhs, chunks):
                    pairs = [(c, a, b) for c in chunks for a, b in ((0, 0), (0, 1), (1, 0))]
                    for i, (c, a, b) in enumerate(pairs):
                        last = nc.tensor.matmul(dst, lhs(a, c), rhs(b, c), start=(i == 0), stop=(i == len(pairs) - 1))
                    return last

                w = (w_hi, w_lo)

                def gate_up(n, q, T, first):
                    r = q % 2
                    if q == 0:
                        pe.wait_ge(rotated, T * 2 + 2)
                    if not first:
                        pe.wait_ge(h_done, n - 1)
                    passes(g_ps[r][:, 0:QF], lambda a, c: xT[a][:, c, :],
                           lambda b, c: w[b][:, gu_cols(q, 0, c)], range(KC)).then_inc(g_done, 1)
                    passes(u_ps[r][:, 0:QF], lambda a, c: xT[a][:, c, :],
                           lambda b, c: w[b][:, gu_cols(q, 1, c)], range(KC)).then_inc(u_done, 1)

                def turn(n, q):
                    r = q % 2
                    pe.wait_ge(h_done, n + 1)
                    for j in range(QJ):
                        last = nc.tensor.transpose(hT_ps[r][:, j * P:(j + 1) * P], hh[r][:, j * P:(j + 1) * P], ident[:])
                    last.then_inc(hT_done, 1)

                def down(n, q, t):
                    r = q % 2
                    pe.wait_ge(hi_done, n + 1)
                    pe.wait_ge(lo_done, n + 1)
                    if q == 0:
                        pe.wait_ge(y_free, t + 1)
                    for j in range(QJ):
                        for i, (a, b) in enumerate(((0, 0), (0, 1), (1, 0))):
                            last = nc.tensor.matmul(y_ps[:, 0:D], hT[r][a][:, j * P:(j + 1) * P], w[b][:, d_cols(q, j)],
                                                    start=(q == 0 and j == 0 and i == 0),
                                                    stop=(q == QUADS - 1 and j == QJ - 1 and i == 2))
                    last.then_inc(d_done, 1)

                def turn_outputs(T, first=False):
                    pe.wait_ge(ot_loaded, T * 16 + 16)
                    if not first:
                        pe.wait_ge(simrow_ready, T)
                    for g in range(GPB):
                        last = nc.tensor.transpose(m_ps[:, g * P:(g + 1) * P], ot[:, g, :], ident[:])
                    last.then_inc(oT_done, 1)

                def turn_attn(T):
                    pe.wait_ge(attn_ready, T + 1)
                    for c in range(KC):
                        last = nc.tensor.transpose(m_ps[:, c * P:(c + 1) * P], attn[:, c * P:(c + 1) * P], ident[:])
                    last.then_inc(aT_done, 1)

                def project_out(T):
                    pe.wait_ge(aT_lo, T + 1)
                    passes(m_ps[:, 0:D], lambda a, c: aT[a][:, c, :], lambda b, c: wo[b][:, c, :],
                           range(KC)).then_inc(wo_done, 1)

                def turn_x1(T):
                    pe.wait_ge(x1n_ready, T + 1)
                    for c in range(KC):
                        last = nc.tensor.transpose(m_ps[:, c * P:(c + 1) * P], x1n[:, c * P:(c + 1) * P], ident[:])
                    last.then_inc(xT_done, 1)

                def route(T):
                    pe.wait_ge(xT_lo, T + 1)
                    passes(m_ps[:, 0:E], lambda a, c: xTn[a][:, c, :], lambda b, c: gate[b][:, c, :],
                           range(KC)).then_inc(logits_done, 1)

                def turn_onehots(T):
                    pe.wait_ge(oh_ready, T + 1)
                    nc.tensor.transpose(m_ps[:, 0:P], oh[:, SEL:TOPK, :].rearrange("p k e -> p (k e)"),
                                        ident[:]).then_inc(ohT_done, 1)

                def similar(T):
                    pe.wait_ge(ohT_ready, T + 1)
                    nc.tensor.matmul(m_ps[:, 0:P], ohT[:], simb[:], start=True, stop=True).then_inc(sim_done, 1)

                pe.wait_ge(set_up, SETUP)
                turn_outputs(0, True)
                for piece in (turn_attn, project_out, turn_x1, route, turn_onehots, similar):
                    piece(0)
                gate_up(0, 0, 0, True)
                gate_up(1, 1, 0, True)
                turn(0, 0)
                with pe.Fori(0, TILES) as t:
                    for s in range(QUADS):
                        n = t * QUADS + s + 2
                        gate_up(n, (s + 2) % QUADS, t + (s + 2) // QUADS, False)
                        if s == 0:
                            turn_outputs(t + 1)
                        if s == 1:
                            turn_attn(t + 1)
                        if s == 3:
                            route(t + 1)
                        turn(n - 1, (s + 1) % QUADS)
                        if s == 4:
                            turn_onehots(t + 1)
                        down(n - 2, s, t)
                        if s == 1:
                            project_out(t + 1)
                        if s == 2:
                            turn_x1(t + 1)
                        if s == 4:
                            similar(t + 1)

            @block.scalar
            def _(act):
                def tanh(n, r, first):
                    act.wait_ge(g_done, n + 1)
                    if not first:
                        act.wait_ge(a_done, n - 1)
                    nc.scalar.activation(th[r][:], g_ps[r][:, 0:QF], ACT.Tanh, scale=0.5).then_inc(tanh_done, 1)

                def high(n, r):
                    act.wait_ge(hT_done, n + 1)
                    nc.scalar.copy(hT[r][0][:], hT_ps[r][:, 0:QF]).then_inc(hi_done, 1)

                def attn_high(T):
                    act.wait_ge(aT_done, T + 1)
                    nc.scalar.copy(aT[0][:].rearrange("p c n -> p (c n)"), m_ps[:, 0:D]).then_inc(aT_hi, 1)

                def x1_high(T):
                    act.wait_ge(xT_done, T + 1)
                    nc.scalar.copy(xTn[0][:].rearrange("p c n -> p (c n)"), m_ps[:, 0:D]).then_inc(xT_hi, 1)

                def exps(T):
                    act.wait_ge(nmax_ready, T + 1)
                    nc.scalar.activation(ex[:], m_ps[:, 0:E], ACT.Exp, bias=nmax[:], accum_out=esum[:]).then_inc(ex_done, 1)

                def onehots_out(T):
                    act.wait_ge(ohT_done, T + 1)
                    nc.scalar.copy(ohT[:], m_ps[:, 0:P]).then_inc(ohT_ready, 1)

                def similar_out(T):
                    act.wait_ge(sim_done, T + 1)
                    nc.scalar.copy(simrow[:].rearrange("p s e -> p (s e)"), m_ps[:, 0:P]).then_inc(simrow_ready, 1)

                def rotate(T):
                    act.wait_ge(xT_lo, T + 1)
                    for i in range(2):
                        nc.scalar.copy(xT[i][:], xTn[i][:].bitcast(F32)).then_inc(rotated, 1)

                for piece in (attn_high, x1_high, exps, onehots_out, similar_out, rotate):
                    piece(0)
                tanh(0, 0, True)
                tanh(1, 1, True)
                high(0, 0)
                with act.Fori(0, TILES) as t:
                    for s in range(QUADS):
                        n = t * QUADS + s + 2
                        tanh(n, s % 2, False)
                        if s == 1:
                            attn_high(t + 1)
                        if s == 5:
                            act.wait_ge(u_done, n + 1)
                            rotate(t + 1)
                        high(n - 1, (s + 1) % 2)
                        if s == 4:
                            onehots_out(t + 1)
                        if s == 2:
                            x1_high(t + 1)
                        if s == 3:
                            exps(t + 1)
                        if s == 4:
                            similar_out(t + 1)

            @block.vector
            def _(dve):
                nc.vector.memset(simb[:], 0.0).then_inc(sim_zero, 1)
                nc.vector.memset(ones[:], 1.0).then_inc(set_up, 1)
                nc.vector.memset(half_pow[:], -0.5).then_inc(set_up, 1)
                nc.vector.memset(pace[:], 0.0).then_inc(y_free, 1)
                nc.vector.memset(ob[:], 0.0).then_inc(out_stored, 16)
                dve.wait_ge(consts, 16 * 9)
                nc.vector.tensor_copy(wo[0][:], wo_f[:]).then_inc(set_up, 1)
                nc.vector.tensor_copy(gate[0][:], gate_f[:]).then_inc(set_up, 1)
                dve.wait_ge(set_up, 4)
                nc.vector.tensor_tensor(wo[1][:], wo_f[:], wo[0][:].bitcast(F32), ALU.subtract).then_inc(set_up, 1)
                nc.vector.tensor_tensor(gate[1][:], gate_f[:], gate[0][:].bitcast(F32), ALU.subtract).then_inc(set_up, 1)
                nc.vector.copy_predicated(simb[:], ident[:].bitcast(U32), ones[:]).then_inc(set_up, 1)
                nc.vector.memset(coef[:], 0.0).then_inc(set_up, 1)
                dve.wait_ge(set_up, SETUP)

                count = [0]
                base = [0]

                def link(ins):
                    count[0] += 1
                    ins.then_inc(chain, 1)
                    return base[0] + count[0]

                def then(value):
                    dve.wait_ge(chain, value)

                def then_plain(value):
                    dve.wait_ge(chain, value)
                    nc.vector.memset(pace[:], 0.0)

                def gated(n, r, first):
                    dve.wait_ge(tanh_done, n + 1)
                    if not first:
                        dve.wait_ge(c_done, n - 1)
                    nc.vector.scalar_tensor_tensor(hg[r][:], th[r][:], 1.0, g_ps[r][:, 0:QF], ALU.add,
                                                   ALU.mult).then_inc(a_done, 1)

                def hidden(n, r, first):
                    dve.wait_ge(c_done, n + 1)
                    dve.wait_ge(u_done, n + 1)
                    if not first:
                        dve.wait_ge(hT_done, n - 1)
                    nc.vector.tensor_tensor(hh[r][:], hc[r][:], u_ps[r][:, 0:QF], ALU.mult).then_inc(h_done, 1)

                def low(n, r):
                    dve.wait_ge(hi_done, n + 1)
                    nc.vector.tensor_tensor(hT[r][1][:], hT_ps[r][:, 0:QF], hT[r][0][:].bitcast(F32),
                                            ALU.subtract).then_inc(lo_done, 1)

                def normalise(T):
                    m = m_ps[:].rearrange("p (g h r) -> p g h r", g=GPB, h=GH)
                    dve.wait_ge(oT_done, T + 1)
                    k = link(nc.vector.reciprocal(rsum[:], m[:, :, :, HD]))
                    then(k)
                    nc.vector.tensor_tensor(attn[:].rearrange("p (g h d) -> p g h d", g=GPB, h=GH), m[:, :, :, 0:HD],
                                            rsum[:].unsqueeze(3).to_broadcast([P, GPB, GH, HD]),
                                            ALU.mult).then_inc(attn_ready, 1)

                def attn_low(T):
                    dve.wait_ge(aT_hi, T + 1)
                    nc.vector.tensor_tensor(aT[1][:].rearrange("p c n -> p (c n)"), m_ps[:, 0:D],
                                            aT[0][:].rearrange("p c n -> p (c n)").bitcast(F32),
                                            ALU.subtract).then_inc(aT_lo, 1)

                def norm(src, src_sem, value, st, m, ve, ve_sem, rs, rs_sem, turn, dst, dst_sem, before=None):
                    dve.wait_ge(src_sem, value)
                    k = link(nc.vector.bn_stats(st[:], src[:]))
                    then_plain(k)
                    k = link(nc.vector.bn_aggr(m[:], st[:]))
                    then(k)
                    nc.vector.tensor_scalar(ve[:], m[:, 1:2], EPS, None, ALU.add).then_inc(ve_sem, 1)
                    dve.wait_ge(rs_sem, turn)
                    if before is not None:
                        dve.wait_ge(*before)
                    nc.vector.tensor_scalar(dst[:], src[:], m[:, 0:1], rs[:], ALU.subtract, ALU.mult).then_inc(dst_sem, 1)

                def first_norm(T):
                    dve.wait_ge(wo_done, T + 1)
                    dve.wait_ge(xt_loaded, T * 16 + 16)
                    nc.vector.tensor_tensor(z[:], m_ps[:, 0:D], xt[:], ALU.add).then_inc(z_done, 1)
                    norm(z, z_done, T + 1, stats, mv, veps, veps_ready, rstd, rstd_ready, T + 1, x1n, x1n_ready)

                def x1_low(T):
                    dve.wait_ge(xT_hi, T + 1)
                    nc.vector.tensor_tensor(xTn[1][:].rearrange("p c n -> p (c n)"), m_ps[:, 0:D],
                                            xTn[0][:].rearrange("p c n -> p (c n)").bitcast(F32),
                                            ALU.subtract).then_inc(xT_lo, 1)

                def logits_max(T):
                    dve.wait_ge(logits_done, T + 1)
                    nc.vector.tensor_reduce(nmax[:], m_ps[:, 0:E], AX.X, ALU.max, negate=True).then_inc(nmax_ready, 1)

                def top_experts(T):
                    dve.wait_ge(ex_done, T + 1)
                    k = link(nc.vector.reciprocal(re[:], esum[:]))
                    then(k)
                    k = link(nc.vector.tensor_scalar(probs[:], ex[:], re[:], None, ALU.mult))
                    then_plain(k)
                    k = link(nc.vector.max(top[:], probs[:]))
                    then(k)
                    k = link(nc.vector.reduce_sum(wsum[:], top[:], AX.X))
                    ki = link(nc.vector.max_index(idx[:], top[:], probs[:]))
                    then(ki)
                    ki = link(nc.vector.tensor_copy(idxf[:], idx[:]))
                    k = link(nc.vector.tensor_scalar(wclip[:], wsum[:], 1e-12, None, ALU.max))
                    then(ki)
                    nc.vector.tensor_tensor(oh[:], iota[:].unsqueeze(1).to_broadcast([P, TOPK, E]),
                                            idxf[:].unsqueeze(2).to_broadcast([P, TOPK, E]),
                                            ALU.is_equal).then_inc(oh_ready, 1)
                    then(k)
                    k = link(nc.vector.reciprocal(winv[:], wclip[:]))
                    then(k)
                    link(nc.vector.tensor_scalar(w8[:], top[:], winv[:], 0.5, ALU.mult, ALU.mult))

                def nearest(T):
                    dve.wait_ge(prod_done, T + 1)
                    k = link(nc.vector.reduce_sum(cand[:], prod[:], AX.X))
                    then(k)
                    k = link(nc.vector.tensor_reduce(best[:], cand[:], AX.X, ALU.max))
                    then(k)
                    link(nc.vector.tensor_scalar(keep[:], best[:], THRESH, None, ALU.is_lt))
                    return link(nc.vector.tensor_tensor(eq[:], cand[:], best[:].unsqueeze(2).to_broadcast([P, SEL, SEL]),
                                                        ALU.is_equal))

                def coefficients(k):
                    then(k)
                    link(nc.vector.tensor_tensor(coef[:, SEL:TOPK], keep[:], w8[:, SEL:TOPK], ALU.mult))
                    k = link(nc.vector.tensor_tensor(wt[:], eq[:], rankw[:].unsqueeze(1).to_broadcast([P, SEL, SEL]),
                                                     ALU.mult))
                    then(k)
                    link(nc.vector.tensor_tensor(move[:], w8[:, SEL:TOPK], coef[:, SEL:TOPK], ALU.subtract))
                    k = link(nc.vector.tensor_reduce(wm[:], wt[:], AX.X, ALU.max))
                    then(k)
                    k = link(nc.vector.tensor_tensor(sel[:], wt[:], wm[:].unsqueeze(2).to_broadcast([P, SEL, SEL]),
                                                     ALU.is_equal))
                    then(k)
                    k = link(nc.vector.tensor_tensor(moved[:], sel[:], move[:].unsqueeze(2).to_broadcast([P, SEL, SEL]),
                                                     ALU.mult))
                    then(k)
                    k = link(nc.vector.reduce_sum(added[:], moved[:].rearrange("p s q -> p q s"), AX.X))
                    then(k)
                    nc.vector.tensor_tensor(coef[:, 0:SEL], added[:], w8[:, 0:SEL], ALU.add).then_inc(coef_ready, 1)

                def combine(T, used):
                    dve.wait_ge(prod2_done, T + 1)
                    if used is not None:
                        dve.wait_ge(c_done, used)
                    nc.vector.reduce_sum(cw[:], prod2[:].rearrange("p k e -> p e k"), AX.X).then_inc(cw_ready, 1)

                for piece in (normalise, attn_low, first_norm, x1_low, logits_max, top_experts):
                    piece(0)
                coefficients(nearest(0))
                combine(0, None)
                k = link(nc.vector.tensor_copy(x1[:], x1n[:]))
                then(k)
                gated(0, 0, True)
                hidden(0, 0, True)
                gated(1, 1, True)
                low(0, 0)
                hidden(1, 1, True)
                before = count[0]
                count[0] = 0
                per = CHAIN
                with dve.Fori(0, TILES) as t:
                    base[0] = t * per + before
                    for s in range(QUADS):
                        n = t * QUADS + s + 2
                        gated(n, s % 2, False)
                        if s == 0:
                            normalise(t + 1)
                        if s == 1:
                            attn_low(t + 1)
                        if s == 3:
                            logits_max(t + 1)
                        if s == 5:
                            k = nearest(t + 1)
                        low(n - 1, (s + 1) % 2)
                        hidden(n, s % 2, False)
                        if s == 1:
                            first_norm(t + 1)
                        if s == 2:
                            x1_low(t + 1)
                        if s == 3:
                            top_experts(t + 1)
                        if s == 5:
                            coefficients(k)
                            combine(t + 1, t * QUADS + QUADS)
                        if s == QUADS - 1:
                            dve.wait_ge(d_done, t * QUADS + QUADS)
                            nc.vector.tensor_tensor(r2[:], y_ps[:, 0:D], x1[:], ALU.add).then_inc(y_free, 1)
                            norm(r2, y_free, t + 2, stats2, mv2, veps2, veps2_ready, rstd2, rstd2_ready, t + 1, ob,
                                 out_ready, before=(out_stored, t * 16 + 16))
                            k = link(nc.vector.tensor_copy(x1[:], x1n[:]))
                    assert count[0] == per, (count[0], before)

            @block.gpsimd
            def _(pool):
                def weighted(n, r, q, first):
                    pool.wait_ge(a_done, n + 1)
                    if not first:
                        pool.wait_ge(h_done, n - 1)
                    v = lambda tile: tile[:].rearrange("p (e f) -> p e f", f=FF)
                    nc.gpsimd.tensor_tensor(v(hc[r]), v(hg[r]),
                                            cw[:, q * QE:(q + 1) * QE].unsqueeze(2).to_broadcast([P, QE, FF]),
                                            ALU.mult).then_inc(c_done, 1)

                def power(ve, ve_sem, rs, rs_sem, value):
                    pool.wait_ge(ve_sem, value)
                    nc.gpsimd.tensor_tensor(rs[:], ve[:], half_pow[:], ALU.pow).then_inc(rs_sem, 1)

                def candidates(T):
                    pool.wait_ge(simrow_ready, T + 1)
                    nc.gpsimd.tensor_tensor(prod[:], simrow[:].unsqueeze(2).to_broadcast([P, SEL, SEL, E]),
                                            oh[:, 0:SEL, :].unsqueeze(1).to_broadcast([P, SEL, SEL, E]),
                                            ALU.mult).then_inc(prod_done, 1)

                def spread(T):
                    pool.wait_ge(coef_ready, T + 1)
                    nc.gpsimd.tensor_tensor(prod2[:], oh[:], coef[:].unsqueeze(2).to_broadcast([P, TOPK, E]),
                                            ALU.mult).then_inc(prod2_done, 1)

                pool.wait_ge(set_up, SETUP)
                power(veps, veps_ready, rstd, rstd_ready, 1)
                candidates(0)
                spread(0)
                pool.wait_ge(cw_ready, 1)
                weighted(0, 0, 0, True)
                weighted(1, 1, 1, True)
                with pool.Fori(0, TILES) as t:
                    for s in range(QUADS):
                        n = t * QUADS + s + 2
                        if s == QUADS - 2:
                            pool.wait_ge(cw_ready, t + 2)
                        weighted(n, s % 2, (s + 2) % QUADS, False)
                        if s == 1:
                            power(veps, veps_ready, rstd, rstd_ready, t + 2)
                        if s == 4:
                            candidates(t + 1)
                        if s == 5:
                            spread(t + 1)
                        if s == QUADS - 1:
                            power(veps2, veps2_ready, rstd2, rstd2_ready, t + 1)


_INS = ["xT", "x", "Wq", "Wk", "Wv", "Wo", "gateT", "guT", "dT", "sim", "ident", "iota", "rankw", "maskS", "maskST"]


def laid_out(i):
    import numpy as np
    a = {k: np.asarray(v) for k, v in i.items()}
    x = np.ascontiguousarray(a["L0_attn_x"].reshape(N, D))
    gu = a["L0_ffn_gate_up_proj"].reshape(QUADS, QE, 2, FF, KC, P)
    dn = a["L0_ffn_down_proj"].transpose(0, 2, 1).reshape(QUADS, QJ, P, D)
    keys, queries = np.arange(P)[None, :], np.arange(P)[:, None]
    return {
        "xT": np.ascontiguousarray(x.reshape(N, KC, P).transpose(2, 1, 0)),
        "x": x,
        "Wq": np.ascontiguousarray(a["L0_attn_Wq"].reshape(D, GPB, GH, HD).transpose(0, 1, 3, 2).reshape(D, D)),
        "Wk": np.ascontiguousarray(a["L0_attn_Wk"]),
        "Wv": np.ascontiguousarray(a["L0_attn_Wv"]),
        "Wo": np.ascontiguousarray(a["L0_attn_Wo"]),
        "gateT": np.ascontiguousarray(a["L0_ffn_gate_weight"].T),
        "guT": np.ascontiguousarray(gu.transpose(5, 0, 2, 4, 1, 3).reshape(P, QUADS, GUW)),
        "dT": np.ascontiguousarray(dn.transpose(2, 0, 1, 3).reshape(P, QUADS, QJ * D)),
        "sim": np.ascontiguousarray(a["L0_ffn_similarity"]),
        "ident": np.eye(P, dtype=np.float32),
        "iota": np.ascontiguousarray(np.broadcast_to(np.arange(E, dtype=np.float32), (P, E))),
        "rankw": np.ascontiguousarray(np.broadcast_to(np.arange(SEL, 0, -1, dtype=np.float32), (P, SEL))),
        "maskS": np.where(keys > queries, np.float32(NEG), np.float32(0)).astype(np.float32),
        "maskST": np.where(keys < queries, np.float32(NEG), np.float32(0)).astype(np.float32),
    }


def kernel(**inputs):
    import concourse.bacc as bacc
    from concourse.bass_utils import run_bass_kernel_spmd

    arrays = laid_out(inputs)
    nc = bacc.Bacc("TRN2", target_bir_lowering=False, num_devices=1)
    args = [nc.dram_tensor(f"in_{k}", arrays[k].shape, F32, kind="ExternalInput").ap() for k in _INS]
    out = nc.dram_tensor("out", (N, D), F32, kind="ExternalOutput").ap()
    moe_block(nc, *args, out)
    r = run_bass_kernel_spmd(nc, [{f"in_{k}": arrays[k] for k in _INS}], core_ids=[0])
    return r.results[0]["out"].reshape(B, T, D)
```
